# Optimizing a Trainium2 kernel written in Bass

```python
import numpy as np
import jax
import jax.numpy as jnp

def _softmax(x, axis=-1):
    return jax.nn.softmax(x, axis=axis)

def _gelu(x):
    return jax.nn.gelu(x, approximate=True)

def _silu(x):
    return jax.nn.silu(x)

def _sigmoid(x):
    return jax.nn.sigmoid(x)

def _layernorm(x, axis=-1, eps=1e-05):
    m = jnp.mean(x, axis=axis, keepdims=True)
    v = jnp.var(x, axis=axis, keepdims=True)
    return (x - m) / jnp.sqrt(v + eps)

def _scatter_add(tgt, idx, src, axis=0):
    return tgt.at[idx].add(src)

def _segment_sum(src, seg, n):
    return jax.ops.segment_sum(src, seg, n)
kernel_name = 'mk_hybrid_d1_jaxref_r8_0067f2'

def setup_inputs(seed: int=0):
    np.random.seed(seed)
    _w = jnp.asarray

    def _L0_attn_a_setup():
        import jax, jax.numpy as jnp
        import numpy as np
        FOCUS = 3
        EPS = 1e-06

        def _norm_last(t):
            return t / jnp.sum(t, axis=-1, keepdims=True)
        key = jax.random.key(seed)
        ks = jax.random.split(key, 6)
        B, N, C = (4, 512, 128)
        s = 0.02
        return {'x': jax.random.normal(ks[0], (B, N, C), jnp.float32), 'w_qkv': jax.random.normal(ks[1], (3 * C, C), jnp.float32) * s, 'w_proj': jax.random.normal(ks[2], (C, C), jnp.float32) * s, 'b_proj': jax.random.normal(ks[3], (C,), jnp.float32) * s, 'w_dwc': jax.random.normal(ks[4], (C, 3), jnp.float32) * s, 'b_dwc': jax.random.normal(ks[5], (C,), jnp.float32) * s}
    _L0_attn_a_in = _L0_attn_a_setup()

    def _L0_attn_b_setup():
        import jax, jax.numpy as jnp
        import numpy as np
        TAU_INV = 0.5
        V_TH = 1.0
        DECAY = 0.9
        ATAN_ALPHA = 2.0
        LN_EPS = 1e-05

        @jax.custom_vjp
        def spike(x):
            return (x >= 0.0).astype(x.dtype)

        def _spike_fwd(x):
            return (spike(x), x)

        def _spike_bwd(x, g):
            sg = ATAN_ALPHA * 0.5 / (1.0 + (jnp.pi * 0.5 * ATAN_ALPHA * x) ** 2)
            return (g * sg,)
        spike.defvjp(_spike_fwd, _spike_bwd)

        def lif_step(v, x_t):
            v = v + (x_t - v) * TAU_INV
            s = spike(v - V_TH)
            v = v * (1.0 - s)
            return (v, s)

        def lif_scan(x):
            xT = jnp.swapaxes(x, 0, 1)
            _, sT = jax.lax.scan(lif_step, jnp.zeros_like(xT[0]), xT)
            return jnp.swapaxes(sT, 0, 1)

        def layernorm(x, g, b):
            mu = jnp.mean(x, axis=-1, keepdims=True)
            var = jnp.mean((x - mu) ** 2, axis=-1, keepdims=True)
            return (x - mu) * jax.lax.rsqrt(var + LN_EPS) * g + b

        def srwkv_forward(x, Wr, Wk, Wv, Wo, W1, b1, W2, b2, ln1_g, ln1_b, ln2_g, ln2_b):
            residual = x
            R = jnp.einsum('btd,ed->bte', x, Wr)
            K = jnp.einsum('btd,ed->bte', x, Wk)
            V = jnp.einsum('btd,ed->bte', x, Wv)
            RT = jnp.swapaxes(R, 0, 1)
            KT = jnp.swapaxes(K, 0, 1)
            VT = jnp.swapaxes(V, 0, 1)
            B, _, D = x.shape
            z = jnp.zeros((B, D), dtype=x.dtype)

            def step(carry, inp):
                h, vr, vk, vv = carry
                r_in, k_in, v_in = inp
                vr, r = lif_step(vr, r_in)
                vk, k = lif_step(vk, k_in)
                vv, v = lif_step(vv, v_in)
                h = h * DECAY + k * v
                y = r * h
                return ((h, vr, vk, vv), y)
            _, yT = jax.lax.scan(step, (z, z, z, z), (RT, KT, VT))
            attn_out = jnp.einsum('tbd,ed->bte', yT, Wo)
            x1 = layernorm(residual + attn_out, ln1_g, ln1_b)
            h1 = jnp.einsum('btd,fd->btf', x1, W1) + b1
            s1 = lif_scan(h1)
            h2 = jnp.einsum('btf,df->btd', s1, W2) + b2
            ffn_out = lif_scan(h2)
            return layernorm(x1 + ffn_out, ln2_g, ln2_b)
        key = jax.random.key(seed)
        ks = jax.random.split(key, 8)
        B, T, D, F = (8, 128, 128, 512)
        s_d = 1.0 / np.sqrt(D)
        s_f = 1.0 / np.sqrt(F)
        return {'x': jax.random.normal(ks[0], (B, T, D), jnp.float32), 'Wr': jax.random.normal(ks[1], (D, D), jnp.float32) * s_d, 'Wk': jax.random.normal(ks[2], (D, D), jnp.float32) * s_d, 'Wv': jax.random.normal(ks[3], (D, D), jnp.float32) * s_d, 'Wo': jax.random.normal(ks[4], (D, D), jnp.float32) * s_d, 'W1': jax.random.normal(ks[5], (F, D), jnp.float32) * s_d, 'b1': jnp.zeros((F,), jnp.float32), 'W2': jax.random.normal(ks[6], (D, F), jnp.float32) * s_f, 'b2': jnp.zeros((D,), jnp.float32), 'ln1_g': jnp.ones((D,), jnp.float32), 'ln1_b': jnp.zeros((D,), jnp.float32), 'ln2_g': jnp.ones((D,), jnp.float32), 'ln2_b': jnp.zeros((D,), jnp.float32)}
    _L0_attn_b_in = _L0_attn_b_setup()

    def _L0_ffn_setup():
        import jax, jax.numpy as jnp
        import numpy as np
        DIM = 128
        HID = 256
        E = 8
        K = 2
        key = jax.random.key(seed)
        ks = jax.random.split(key, 5)
        s_in = 1.0 / np.sqrt(DIM)
        s_hid = 1.0 / np.sqrt(HID)
        x = jax.random.normal(ks[0], (2, 256, DIM), dtype=jnp.float32)
        Wg = jax.random.uniform(ks[1], (DIM, E), minval=-s_in, maxval=s_in, dtype=jnp.float32)
        W1 = jax.random.uniform(ks[2], (E, DIM, HID), minval=-s_in, maxval=s_in, dtype=jnp.float32)
        W3 = jax.random.uniform(ks[3], (E, DIM, HID), minval=-s_in, maxval=s_in, dtype=jnp.float32)
        W2 = jax.random.uniform(ks[4], (E, HID, DIM), minval=-s_hid, maxval=s_hid, dtype=jnp.float32)
        return {'x': x, 'Wg': Wg, 'W1': W1, 'W3': W3, 'W2': W2}
    _L0_ffn_in = _L0_ffn_setup()
    _d = {'L0_attn_a_x': _L0_attn_a_in['x'], 'L0_attn_a_w_qkv': _L0_attn_a_in['w_qkv'], 'L0_attn_a_w_proj': _L0_attn_a_in['w_proj'], 'L0_attn_a_b_proj': _L0_attn_a_in['b_proj'], 'L0_attn_a_w_dwc': _L0_attn_a_in['w_dwc'], 'L0_attn_a_b_dwc': _L0_attn_a_in['b_dwc'], 'L0_attn_b_Wr': _L0_attn_b_in['Wr'], 'L0_attn_b_Wk': _L0_attn_b_in['Wk'], 'L0_attn_b_Wv': _L0_attn_b_in['Wv'], 'L0_attn_b_Wo': _L0_attn_b_in['Wo'], 'L0_attn_b_W1': _L0_attn_b_in['W1'], 'L0_attn_b_b1': _L0_attn_b_in['b1'], 'L0_attn_b_W2': _L0_attn_b_in['W2'], 'L0_attn_b_b2': _L0_attn_b_in['b2'], 'L0_attn_b_ln1_g': _L0_attn_b_in['ln1_g'], 'L0_attn_b_ln1_b': _L0_attn_b_in['ln1_b'], 'L0_attn_b_ln2_g': _L0_attn_b_in['ln2_g'], 'L0_attn_b_ln2_b': _L0_attn_b_in['ln2_b'], 'L0_ffn_Wg': _L0_ffn_in['Wg'], 'L0_ffn_W1': _L0_ffn_in['W1'], 'L0_ffn_W3': _L0_ffn_in['W3'], 'L0_ffn_W2': _L0_ffn_in['W2']}
    _x0 = _d['L0_attn_a_x']
    _d['L0_attn_a_x'] = jax.random.normal(jax.random.fold_in(jax.random.key(seed), 1), (8, 512, 128), dtype=_x0.dtype)
    del _x0
    return _d

def reference(L0_attn_a_x, L0_attn_a_w_qkv, L0_attn_a_w_proj, L0_attn_a_b_proj, L0_attn_a_w_dwc, L0_attn_a_b_dwc, L0_attn_b_Wr, L0_attn_b_Wk, L0_attn_b_Wv, L0_attn_b_Wo, L0_attn_b_W1, L0_attn_b_b1, L0_attn_b_W2, L0_attn_b_b2, L0_attn_b_ln1_g, L0_attn_b_ln1_b, L0_attn_b_ln2_g, L0_attn_b_ln2_b, L0_ffn_Wg, L0_ffn_W1, L0_ffn_W3, L0_ffn_W2):

    def _L0_attn_a_ref(x, w_qkv, w_proj, b_proj, w_dwc, b_dwc):
        import jax, jax.numpy as jnp
        import numpy as np
        FOCUS = 3
        EPS = 1e-06

        def _norm_last(t):
            return t / jnp.sum(t, axis=-1, keepdims=True)
        B, N, C = x.shape
        H = 16
        d = C // H
        qkv = jnp.einsum('bnc,oc->bno', x, w_qkv).reshape(B, N, 3, H, d)
        qkv = jnp.transpose(qkv, (2, 0, 3, 1, 4))
        q, k, v = (qkv[0], qkv[1], qkv[2])
        q = _norm_last(jax.nn.relu(q) + EPS)
        k = _norm_last(jax.nn.relu(k) + EPS)
        q = _norm_last(q ** FOCUS)
        k = _norm_last(k ** FOCUS)
        kv = jnp.einsum('bhnd,bhne->bhde', k, v)
        z = 1.0 / (jnp.einsum('bhnd,bhd->bhn', q, k.sum(axis=2)) + EPS)
        out = jnp.einsum('bhnd,bhde,bhn->bhne', q, kv, z)
        out = jnp.transpose(out, (0, 2, 1, 3)).reshape(B, N, C)
        xp = jnp.pad(out, ((0, 0), (1, 1), (0, 0)))
        conv = xp[:, 0:N, :] * w_dwc[:, 0] + xp[:, 1:N + 1, :] * w_dwc[:, 1] + xp[:, 2:N + 2, :] * w_dwc[:, 2] + b_dwc
        out = out + conv
        return jnp.einsum('bnc,oc->bno', out, w_proj) + b_proj

    def _L0_attn_b_ref(x, Wr, Wk, Wv, Wo, W1, b1, W2, b2, ln1_g, ln1_b, ln2_g, ln2_b):
        import jax, jax.numpy as jnp
        import numpy as np
        TAU_INV = 0.5
        V_TH = 1.0
        DECAY = 0.9
        ATAN_ALPHA = 2.0
        LN_EPS = 1e-05

        @jax.custom_vjp
        def spike(x):
            return (x >= 0.0).astype(x.dtype)

        def _spike_fwd(x):
            return (spike(x), x)

        def _spike_bwd(x, g):
            sg = ATAN_ALPHA * 0.5 / (1.0 + (jnp.pi * 0.5 * ATAN_ALPHA * x) ** 2)
            return (g * sg,)
        spike.defvjp(_spike_fwd, _spike_bwd)

        def lif_step(v, x_t):
            v = v + (x_t - v) * TAU_INV
            s = spike(v - V_TH)
            v = v * (1.0 - s)
            return (v, s)

        def lif_scan(x):
            xT = jnp.swapaxes(x, 0, 1)
            _, sT = jax.lax.scan(lif_step, jnp.zeros_like(xT[0]), xT)
            return jnp.swapaxes(sT, 0, 1)

        def layernorm(x, g, b):
            mu = jnp.mean(x, axis=-1, keepdims=True)
            var = jnp.mean((x - mu) ** 2, axis=-1, keepdims=True)
            return (x - mu) * jax.lax.rsqrt(var + LN_EPS) * g + b

        def srwkv_forward(x, Wr, Wk, Wv, Wo, W1, b1, W2, b2, ln1_g, ln1_b, ln2_g, ln2_b):
            residual = x
            R = jnp.einsum('btd,ed->bte', x, Wr)
            K = jnp.einsum('btd,ed->bte', x, Wk)
            V = jnp.einsum('btd,ed->bte', x, Wv)
            RT = jnp.swapaxes(R, 0, 1)
            KT = jnp.swapaxes(K, 0, 1)
            VT = jnp.swapaxes(V, 0, 1)
            B, _, D = x.shape
            z = jnp.zeros((B, D), dtype=x.dtype)

            def step(carry, inp):
                h, vr, vk, vv = carry
                r_in, k_in, v_in = inp
                vr, r = lif_step(vr, r_in)
                vk, k = lif_step(vk, k_in)
                vv, v = lif_step(vv, v_in)
                h = h * DECAY + k * v
                y = r * h
                return ((h, vr, vk, vv), y)
            _, yT = jax.lax.scan(step, (z, z, z, z), (RT, KT, VT))
            attn_out = jnp.einsum('tbd,ed->bte', yT, Wo)
            x1 = layernorm(residual + attn_out, ln1_g, ln1_b)
            h1 = jnp.einsum('btd,fd->btf', x1, W1) + b1
            s1 = lif_scan(h1)
            h2 = jnp.einsum('btf,df->btd', s1, W2) + b2
            ffn_out = lif_scan(h2)
            return layernorm(x1 + ffn_out, ln2_g, ln2_b)
        return srwkv_forward(x, Wr, Wk, Wv, Wo, W1, b1, W2, b2, ln1_g, ln1_b, ln2_g, ln2_b)

    def _L0_ffn_ref(x, Wg, W1, W3, W2):
        import jax, jax.numpy as jnp
        import numpy as np
        DIM = 128
        HID = 256
        E = 8
        K = 2
        orig_shape = x.shape
        xt = x.reshape(-1, x.shape[-1])
        T = xt.shape[0]
        scores = xt @ Wg
        ew, ei = jax.lax.top_k(scores, K)
        ew = jax.nn.softmax(ew, axis=-1)
        combine = jnp.zeros((T, E), dtype=xt.dtype)
        combine = combine.at[jnp.arange(T)[:, None], ei].add(ew)
        out = jnp.zeros_like(xt)
        for e in range(E):
            h = jax.nn.silu(xt @ W1[e]) * (xt @ W3[e])
            out = out + combine[:, e:e + 1] * (h @ W2[e])
        return out.reshape(orig_shape)
    x = L0_attn_a_x
    x = x + _L0_attn_a_ref(_layernorm(x, axis=-1), L0_attn_a_w_qkv, L0_attn_a_w_proj, L0_attn_a_b_proj, L0_attn_a_w_dwc, L0_attn_a_b_dwc)
    x = x + _L0_ffn_ref(_layernorm(x, axis=-1), L0_ffn_Wg, L0_ffn_W1, L0_ffn_W3, L0_ffn_W2)
    x = x + _L0_attn_b_ref(_layernorm(x, axis=-1), L0_attn_b_Wr, L0_attn_b_Wk, L0_attn_b_Wv, L0_attn_b_Wo, L0_attn_b_W1, L0_attn_b_b1, L0_attn_b_W2, L0_attn_b_b2, L0_attn_b_ln1_g, L0_attn_b_ln1_b, L0_attn_b_ln2_g, L0_attn_b_ln2_b)
    x = x + _L0_ffn_ref(_layernorm(x, axis=-1), L0_ffn_Wg, L0_ffn_W1, L0_ffn_W3, L0_ffn_W2)
    return x

_drawn_inputs = setup_inputs


def setup_inputs(seed=0):
    import zlib

    import numpy as np

    out = dict(_drawn_inputs(seed))
    spreads = {'L0_attn_b_b1': (0.0, 0.1),
     'L0_attn_b_b2': (0.0, 0.1),
     'L0_attn_b_ln1_g': (1.0, 0.2),
     'L0_attn_b_ln1_b': (0.0, 0.1),
     'L0_attn_b_ln2_g': (1.0, 0.2),
     'L0_attn_b_ln2_b': (0.0, 0.1)}
    factors = {'L0_attn_a_w_qkv': 6.881,
     'L0_attn_a_w_proj': 5.187,
     'L0_attn_a_w_dwc': 8.0,
     'L0_attn_a_b_dwc': 8.0,
     'L0_attn_b_Wr': 8.0,
     'L0_attn_b_Wk': 8.0,
     'L0_attn_b_Wv': 8.0,
     'L0_attn_b_Wo': 8.0}
    for name, (base, spread) in spreads.items():
        noise = np.random.default_rng([zlib.crc32(name.encode()), seed]).standard_normal(out[name].shape)
        drawn = base * np.exp(spread * noise) if base else spread * noise
        out[name] = jnp.asarray(drawn.astype(out[name].dtype))
    for name, factor in factors.items():
        out[name] = (out[name] * factor).astype(out[name].dtype)
    return out
```

```python
import concourse.bass as bass
from concourse import mybir
from contextlib import ExitStack
from collections import namedtuple


LayerNorm = namedtuple("LayerNorm", "stats mv var rstd has_var has_rstd")
Stages = namedtuple("Stages", "load hand ffn fin scan")


class Steps:

    def __init__(self, eng, sem):
        self.eng, self.sem, self.n, self.base = eng, sem, 0, 0

    def did(self, instruction):
        instruction.then_inc(self.sem, 1)
        self.n += 1

    def settle(self, wait=None):
        if wait:
            wait(self.eng, self.sem, self.base + self.n)
        else:
            self.eng.wait_ge(self.sem, self.base + self.n)


def rounds(eng, steps, start, end, body):
    before = steps.n
    body(start)
    each = steps.n - before
    if end - start > 1:
        with eng.Fori(start + 1, end) as i:
            steps.n, steps.base = before, (i - start) * each
            body(i)
        steps.n, steps.base = before + (end - start) * each, 0


def is_first(i):
    return isinstance(i, int) and i == 0


def build_program(nc, dram):
    fp32 = mybir.dt.float32
    fp32r = mybir.dt.float32r
    bf16 = mybir.dt.bfloat16
    u32 = mybir.dt.uint32
    ALU = mybir.AluOpType
    ACT = mybir.ActivationFunctionType
    AX = mybir.AxisListType.X

    x_in_dram, out_dram = dram["x"], dram["out"]
    B, N, C = x_in_dram.shape
    P = 128
    TILES = N // P
    E, _, HID = dram["W1"].shape
    CHUNKS = HID // P
    F = dram["lif_w1"].shape[1]
    FCH = F // P
    HEADS, HD = 16, 8
    TOP = 2
    LN_EPS, ATT_EPS = 1e-5, 1e-6
    V_TH, DECAY, HALF = 1.0, 0.9, 0.5
    STEPS = P // B
    SUBS = N // STEPS
    PER = 4
    COLS = (3 + FCH + 1) * B
    CA, CB, CC = 0, 3 * B, (3 + FCH) * B
    LAG_B, LAG_C, LAG_G = 2, 4, 5

    ctx = ExitStack()
    with ctx:
        def sb(name, shape, dt=fp32):
            return ctx.enter_context(nc.sbuf_tensor(name, shape, dt))

        def sem(name):
            return ctx.enter_context(nc.semaphore(name))

        experts_f = sb("experts_f", [P, E, 2 * HID])
        experts_hi = sb("experts_hi", [P, E, 2 * HID], fp32r)
        experts_lo = sb("experts_lo", [P, E, 2 * HID], fp32r)
        down_w = sb("down_w", [P, E, CHUNKS, C])
        gate_f = sb("gate_f", [P, E])
        gate_hi = sb("gate_hi", [P, E], fp32r)
        gate_lo = sb("gate_lo", [P, E], fp32r)
        qkv_w = sb("qkv_w", [P, 3 * C])
        proj_w = sb("proj_w", [P, C])
        rkv_w = sb("rkv_w", [P, 3, C])
        wo_w = sb("wo_w", [P, C])
        lif1_w = sb("lif1_w", [P, F])
        lif2_f = sb("lif2_f", [P, FCH, C])
        lif2_rest = sb("lif2_rest", [P, FCH, C])
        lif2_part = sb("lif2_part", [P, 3, FCH, C], bf16)
        ident = sb("ident", [P, P])
        head_mask = sb("head_mask", [P, P])
        expert_no = sb("expert_no", [P, E])
        cols = sb("cols", [P, FCH + 7])
        half_b1 = sb("half_b1", [P, FCH])
        half_b2 = sb("half_b2", [P, 1])
        centre_w = sb("centre_w", [P, 1])
        proj_b = sb("proj_b", [P, C])
        ln2_g = sb("ln2_g", [P, C])
        ln2_b = sb("ln2_b", [P, C])
        minus_half = sb("minus_half", [P, TILES])
        B1, B2, LN1G, LN1B, DW, DWB = 0, FCH, FCH + 1, FCH + 2, FCH + 3, FCH + 6

        res = sb("res", [P, TILES, C])
        resn = sb("resn", [P, TILES, C])
        x_hi = sb("x_hi", [P, N], fp32r)
        x_lo = sb("x_lo", [P, N], fp32r)
        silu = sb("silu", [P, CHUNKS, N])
        hidden = sb("hidden", [P, 2, CHUNKS, N])
        weighted = sb("weighted", [P, 2, TILES, C])
        acc = sb("acc", [P, TILES, C])
        moe_out = sb("moe_out", [P, TILES, C])
        scores = sb("scores", [P, TILES, E])
        best = sb("best", [P, TILES, 8])
        best_no = sb("best_no", [P, TILES, 8], u32)
        best_nof = sb("best_nof", [P, TILES, TOP])
        lead = sb("lead", [P, TILES])
        top_w = sb("top_w", [P, TOP, TILES])
        pick = sb("pick", [P, TOP, TILES, E])
        comb = sb("comb", [P, TILES, E])

        def ln_set(name, n):
            return LayerNorm(stats=sb(name + "_stats", [P, n, 6]), mv=sb(name + "_mv", [P, n, 2]),
                             var=sb(name + "_var", [P, n]), rstd=sb(name + "_rstd", [P, n]),
                             has_var=sem(name + "_has_var"), has_rstd=sem(name + "_has_rstd"))

        ln_x = ln_set("ln_x", TILES)
        ln_r = ln_set("ln_r", TILES)
        ln_z = ln_set("ln_z", TILES)
        ln_a = ln_set("ln_a", 1)
        ln_g = ln_set("ln_g", 1)
        ln_m = ln_set("ln_m", 1)

        x_tok = sb("x_tok", [P, TILES, C])
        x_plus_b = sb("x_plus_b", [P, TILES, C])
        xn = sb("xn", [P, TILES, C])
        xnT = sb("xnT", [P, N])
        qk = sb("qk", [P, TILES, 2 * HEADS, HD])
        qk2 = sb("qk2", [P, TILES, 2 * HEADS, HD])
        qk_sum = sb("qk_sum", [P, TILES, 2 * HEADS])
        qk_inv = sb("qk_inv", [P, TILES, 2 * HEADS])
        v_one = sb("v_one", [P, TILES, C + 1])
        kv_m = sb("kv_m", [P, C])
        ks_m = sb("ks_m", [P, C])
        qT = sb("qT", [P, N])
        z_inv = sb("z_inv", [P, N])
        att = sb("att", [P, N + 2])
        conv = sb("conv", [P, N])
        z_tok = sb("z_tok", [P, TILES, C])

        lif_in = sb("lif_in", [P, 2, COLS, STEPS])
        lif_u = sb("lif_u", [P, 2, COLS, STEPS])
        lif_v = sb("lif_v", [P, COLS])
        z_ring = sb("z_ring", [P, PER, C])
        x2_ring = sb("x2_ring", [P, PER, C])
        x1T_ring = sb("x1T_ring", [P, PER, P])
        zT = sb("zT", [P, P])
        v_spike = sb("v_spike", [P, B, STEPS])
        kv_in = sb("kv_in", [P, B, STEPS + 1])
        h_out = sb("h_out", [P, B, STEPS + 1])
        h_decay = sb("h_decay", [P, B, STEPS + 1])
        y_fm = sb("y_fm", [P, P])
        x1p = sb("x1p", [P, C])
        x1n = sb("x1n", [P, C])
        s1 = sb("s1", [P, FCH, P], bf16)
        gT = sb("gT", [P, P])
        g_tok = sb("g_tok", [P, C])
        g_n = sb("g_n", [P, C])
        g_s = sb("g_s", [P, C])

        def bank(name):
            return ctx.enter_context(nc.psum_tensor(name, [P, 512], fp32))

        up_banks = [[bank("up_a1"), bank("up_a3")], [bank("up_b1"), bank("up_b3")]]
        down_bank = bank("down_bank")
        side0, side1, side2 = bank("side0"), bank("side1"), bank("side2")

        signals = """
            load_w load_c x_loaded zeros hi_split lo_split
            up_ready silu_done gated down_ready y_weighted added
            xT_ps hi_done lo_done router_ps lead_done top_done comb_done
            xn_done xnT_ps xnT_done qkv_ps qkv_out qk_first cubed qk_done kv_ps kv_masked qT_ps qT_done
            att_ps att_done conv_mid conv_done proj_ps xb_done res_done resn_done
            z_done x2_stored z_stored
            zT_ps zT_done rkv_ps in_a y_done wo_ps x1p_done x1n_done x1T_ps x1T_done lif1_ps in_b
            s1_done lif2_ps in_c g_done g_ps g_copied g_normed x3_done x3n_done
            lif_steps dve_steps act_steps pool_steps out_stored""".split()
        s = namedtuple("Signals", signals)(*[sem(n) for n in signals])

        z_loaded = [sem(f"z_loaded{q}") for q in range(PER)]
        x2_loaded = [sem(f"x2_loaded{q}") for q in range(PER)]

        x2_dram = nc.dram_tensor("x2_scratch", (B, N, C), fp32, kind="Internal").ap()
        z_dram = nc.dram_tensor("z_scratch", (B, N, C), fp32, kind="Internal").ap()

        def rows_of_batch(t, b):
            return t[bass.ds(b, 1)].rearrange("o (j p) c -> p (o j) c", p=P)

        block = ctx.enter_context(nc.Block())
        LOADS_W, LOADS_C = 11, 8
        GROUPS = SUBS // PER


        def wait_apart(eng, which, count):
            if not isinstance(count, int):
                count = eng.to_reg(count)
                eng.wait_ge(s.zeros, 1)
            eng.wait_ge(which, count)

        def stages(t):
            if not isinstance(t, int):
                return Stages(load=True, hand=True, ffn=True, fin=True, scan=True)
            return Stages(load=t + 1 < SUBS, hand=0 <= t - 1 < SUBS, ffn=0 <= t - 3 < SUBS,
                           fin=0 <= t - LAG_G < SUBS, scan=0 <= t < SUBS + LAG_C)

        def upto(n):
            return min(n, SUBS) if isinstance(n, int) else n

        def spiking_block(eng, steps, sub, prepare, experts, finish):
            sub(-1, PER - 1, -1, stages(-1), None)
            sub(0, 0, -1, stages(0), None)

            def group(j, mixed=True, last=False):
                m = B - 2 + j
                for i in range(PER):
                    t = j * PER + 1 + i
                    if last:
                        for e in (2 * i, 2 * i + 1):
                            experts(m, e)
                    else:
                        sub(t, (1 + i) % PER, j, stages(t), (m, 2 * i) if mixed else None)
                prepare(m + 1, j) if not last and not (isinstance(j, int) and j == 0) else None
                finish(m, None if last or (isinstance(j, int) and j == 0) else m + 1, mixed)

            group(0, mixed=False)
            group(1, mixed=False)
            full = (SUBS - 2) // PER
            rounds(eng, steps, 2, full, group)
            for j in range(full, GROUPS + 1):
                group(j)
            group(GROUPS + 1, last=True)

        @block.sync
        def _(sp):
            for dst, src in ((ident[:], dram["ident"]), (head_mask[:], dram["head_mask"]),
                             (expert_no[:], dram["expert_no"]), (cols[:], dram["cols"]),
                             (proj_b[:], dram["b_proj"].partition_broadcast(P)),
                             (ln2_g[:], dram["ln2_g"].partition_broadcast(P)),
                             (ln2_b[:], dram["ln2_b"].partition_broadcast(P)),
                             (qkv_w[:], dram["qkv_w"])):
                sp.dma_start(dst, src).then_inc(s.load_c, 16)

            def load_x(b):
                if not is_first(b):
                    sp.wait_ge(s.xn_done, b)
                    sp.wait_ge(s.xb_done, b)
                sp.dma_start(x_tok[:], rows_of_batch(x_in_dram, b)).then_inc(s.x_loaded, 16)

            load_x(0)
            for dst, src in ((experts_f[:, :, 0:HID], dram["W1"].rearrange("e d h -> d e h")),
                             (experts_f[:, :, HID:], dram["W3"].rearrange("e d h -> d e h")),
                             (down_w[:], dram["W2"].rearrange("e (k p) d -> p e k d", p=P)),
                             (gate_f[:], dram["Wg"]), (proj_w[:], dram["proj_w"]),
                             (rkv_w[:, 0], dram["wr"]), (rkv_w[:, 1], dram["wk"]), (rkv_w[:, 2], dram["wv"]),
                             (wo_w[:], dram["wo"]), (lif1_w[:], dram["lif_w1"]),
                             (lif2_f[:], dram["lif_w2"].rearrange("(k p) d -> p k d", p=P))):
                sp.dma_start(dst, src).then_inc(s.load_w, 16)

            def store_batch(b):
                sp.wait_ge(s.added, b * (E + 1) + E + 1)
                sp.dma_start(rows_of_batch(x2_dram, b), moe_out[:]).then_inc(s.x2_stored, 16)
                sp.wait_ge(s.z_done, b + 1)
                sp.dma_start(rows_of_batch(z_dram, b), z_tok[:]).then_inc(s.z_stored, 16)

            load_x(1)

            def batch(b):
                load_x(b + 2)
                store_batch(b)

            batch(0)
            with sp.Fori(1, B - 2) as b:
                batch(b)
            store_batch(B - 2)
            store_batch(B - 1)

            sp.wait_ge(s.x2_stored, 16 * B)
            sp.wait_ge(s.z_stored, 16 * B)

            def by_time(t, c):
                return t[:, bass.ds(c * STEPS, STEPS), :]

            def tile(t):
                return t

            def load_z(c, slot):
                if not isinstance(c, int) or c >= PER:
                    sp.wait_ge(s.x1p_done, c - PER + 1)
                sp.dma_start(tile(z_ring[:, slot]), by_time(z_dram, c)).then_inc(z_loaded[slot], 16)

            def load_x2(c, slot):
                if not isinstance(c, int) or c >= PER:
                    sp.wait_ge(s.x3_done, c - PER + 1)
                sp.dma_start(tile(x2_ring[:, slot]), by_time(x2_dram, c)).then_inc(x2_loaded[slot], 16)

            def store_out(k):
                sp.wait_ge(s.added, (B + k) * (E + 1) + E + 1)
                for q in range(PER):
                    sp.dma_start(by_time(out_dram, k * PER + q), tile(moe_out[:, q])).then_inc(s.out_stored, 16)

            for c in range(PER):
                load_z(c, c)
            for c in range(PER):
                load_x2(c, c)

            def group(j):
                if not (isinstance(j, int) and j < 4):
                    store_out(j - 4)
                for q in range(PER):
                    load_z(j * PER + q, q)
                    if not (isinstance(j, int) and j < 2):
                        load_x2((j - 1) * PER + q, q)

            for j in range(1, 4):
                group(j)
            with sp.Fori(4, GROUPS) as j:
                group(j)
            store_out(GROUPS - 4)
            for q in range(PER):
                load_x2((GROUPS - 1) * PER + q, q)
            for k in range(GROUPS - 3, GROUPS):
                store_out(k)
            sp.wait_ge(s.out_stored, 16 * SUBS)

        @block.tensor
        def _(pe):
            mm = nc.tensor.matmul

            def three(out, w_hi, w_lo, m_hi, m_lo):
                mm(out, w_lo, m_hi, start=True, stop=False)
                mm(out, w_hi, m_lo, start=False, stop=False)
                return mm(out, w_hi, m_hi, start=False, stop=True)

            def up(m, e):
                for c in range(CHUNKS):
                    if not (is_first(m) and e == 0):
                        pe.wait_ge(s.gated, m * 2 * E + 2 * e + c - 1)
                    for k in range(2):
                        lo = k * HID + c * P
                        three(up_banks[c][k][:, 0:N], experts_hi[:, e, lo:lo + P], experts_lo[:, e, lo:lo + P],
                              x_hi[:], x_lo[:]).then_inc(s.up_ready, 1)

            def down(m, e):
                pe.wait_ge(s.gated, m * 2 * E + 2 * e + 2)
                if not (is_first(m) and e == 0):
                    pe.wait_ge(s.y_weighted, m * E + e)
                for j in range(TILES):
                    for c in range(CHUNKS):
                        last = mm(down_bank[:, j * C:(j + 1) * C], hidden[:, e % 2, c, j * P:(j + 1) * P],
                                  down_w[:, e, c], start=(c == 0), stop=(c == CHUNKS - 1))
                last.then_inc(s.down_ready, 1)

            def router_in(m):
                for j in range(TILES):
                    last = nc.tensor.transpose(side2[:, j * P:(j + 1) * P], resn[:, j], ident[:])
                last.then_inc(s.xT_ps, 1)

            def router(m):
                pe.wait_ge(s.lo_done, m + 1)
                for j in range(TILES):
                    t = slice(j * P, (j + 1) * P)
                    last = three(side0[:, j * E:(j + 1) * E], x_hi[:, t], x_lo[:, t], gate_hi[:], gate_lo[:])
                last.then_inc(s.router_ps, 1)

            def t_x(b):
                pe.wait_ge(s.xn_done, b + 1)
                if not is_first(b):
                    pe.wait_ge(s.lead_done, b)
                for j in range(TILES):
                    last = nc.tensor.transpose(side0[:, j * P:(j + 1) * P], xn[:, j], ident[:])
                last.then_inc(s.xnT_ps, 1)

            def qkv(b, tiles):
                pe.wait_ge(s.xnT_done, b + 1)
                for j in tiles:
                    if j >= 2:
                        pe.wait_ge(s.qkv_out, b * TILES + j - 1)
                    elif not is_first(b):
                        pe.wait_ge(s.lo_done, b)
                    mm((side1, side2)[j % 2][:, 0:3 * C], xnT[:, j * P:(j + 1) * P], qkv_w[:],
                       start=True, stop=True).then_inc(s.qkv_ps, 1)

            def kv(b):
                pe.wait_ge(s.qk_done, b + 1)
                for j in range(TILES):
                    k_tile = qk[:, j, HEADS:2 * HEADS].rearrange("p h d -> p (h d)")
                    last = mm(side0[:, 0:C + 1], k_tile, v_one[:, j], start=(j == 0), stop=(j == TILES - 1))
                last.then_inc(s.kv_ps, 1)
                for j in range(TILES):
                    q_tile = qk[:, j, 0:HEADS].rearrange("p h d -> p (h d)")
                    last = nc.tensor.transpose(side1[:, j * P:(j + 1) * P], q_tile, ident[:])
                last.then_inc(s.qT_ps, 1)

            def attend(b):
                pe.wait_ge(s.kv_masked, b + 1)
                pe.wait_ge(s.qT_done, b + 1)
                mm(side2[:, 0:N], kv_m[:], qT[:], start=True, stop=True)
                mm(side0[:, 0:N], ks_m[:], qT[:], start=True, stop=True).then_inc(s.att_ps, 1)

            def project(b):
                pe.wait_ge(s.conv_done, b + 1)
                for j in range(TILES):
                    last = mm(side1[:, j * C:(j + 1) * C], conv[:, j * P:(j + 1) * P], proj_w[:],
                              start=True, stop=True)
                last.then_inc(s.proj_ps, 1)

            pe.wait_ge(s.load_c, 16 * LOADS_C)
            t_x(0)
            qkv(0, range(TILES))
            kv(0)
            attend(0)
            pe.wait_ge(s.load_w, 16 * LOADS_W)
            project(0)
            pe.wait_ge(s.resn_done, 1)
            router_in(0)
            pe.wait_ge(s.lo_split, 2)
            router(0)

            def batch(b, more=True):
                nothing = lambda: None
                side = [lambda: t_x(b + 1), lambda: qkv(b + 1, (0, 1)), lambda: qkv(b + 1, (2, 3)), nothing,
                        lambda: kv(b + 1), lambda: attend(b + 1), lambda: project(b + 1), nothing]
                for e in range(E):
                    up(b, e)
                    if e:
                        down(b, e - 1)
                    if more:
                        side[e]()
                if more:
                    pe.wait_ge(s.resn_done, b + 2)
                    router_in(b + 1)
                down(b, E - 1)
                if more:
                    router(b + 1)

            batch(0)
            with pe.Fori(1, B - 1) as b:
                batch(b)
            batch(B - 1, False)

            def t_z(t, q, j):
                place = (q + 1) % PER
                pe.wait_ge(z_loaded[place], 16 * (j + (2 if place in (0, 1) else 1)))
                if not (isinstance(t, int) and t < 0):
                    pe.wait_ge(s.in_a, t + 1)
                nc.tensor.transpose(side0[:, 0:P], z_ring[:, place], ident[:]).then_inc(s.zT_ps, 1)

            def t_g(t):
                pe.wait_ge(s.g_done, t - LAG_G + 1)
                if not (isinstance(t, int) and t < LAG_G + 1):
                    pe.wait_ge(s.g_copied, t - LAG_G)
                nc.tensor.transpose(side0[:, P:2 * P], gT[:], ident[:]).then_inc(s.g_ps, 1)

            def rkv(t, on):
                pe.wait_ge(s.zT_done, t + 2)
                if on.fin:
                    pe.wait_ge(s.g_copied, t - LAG_G + 1)
                for k in range(3):
                    last = mm(side0[:, k * P:(k + 1) * P], rkv_w[:, k], zT[:], start=True, stop=True)
                last.then_inc(s.rkv_ps, 1)

            def wo(t):
                pe.wait_ge(s.y_done, t)
                if not (isinstance(t, int) and t < 2):
                    pe.wait_ge(s.x1T_done, t - 1)
                mm(side1[:, 0:C], y_fm[:], wo_w[:], start=True, stop=True).then_inc(s.wo_ps, 1)

            def t_x1(t):
                pe.wait_ge(s.x1n_done, t)
                nc.tensor.transpose(side1[:, 0:P], x1n[:], ident[:]).then_inc(s.x1T_ps, 1)

            def lif1(t, q, on):
                pe.wait_ge(s.x1T_done, t)
                if on.ffn:
                    pe.wait_ge(s.in_c, t - 2)
                elif t > 1:
                    pe.wait_ge(s.in_b, t - 1)
                for k in range(FCH):
                    last = mm(side2[:, k * P:(k + 1) * P], lif1_w[:, k * P:(k + 1) * P], x1T_ring[:, (q - 1) % PER],
                              start=True, stop=True)
                last.then_inc(s.lif1_ps, 1)

            def lif2(t):
                pe.wait_ge(s.s1_done, t - 2)
                pe.wait_ge(s.in_b, upto(t - 1))
                if not (isinstance(t, int) and t < 4):
                    pe.wait_ge(s.in_c, t - 3)
                for k in range(FCH):
                    for part in range(3):
                        last = mm(side2[:, 0:P], lif2_part[:, 2 - part, k], s1[:, k],
                                  start=(k == 0 and part == 0), stop=(k == FCH - 1 and part == 2))
                last.then_inc(s.lif2_ps, 1)

            def sub(t, q, j, on, experts):
                if q == 1 or (isinstance(t, int) and t < 0):
                    pe.wait_ge(s.lead_done, B if isinstance(t, int) and t < PER else B - 1 + j)
                if experts:
                    m, e = experts
                    up(m, e)
                if on.load:
                    t_z(t, q, j)
                if on.fin:
                    t_g(t)
                if on.hand:
                    wo(t)
                if on.ffn:
                    lif2(t)
                if experts and e:
                    down(m, e - 1)
                if on.load:
                    rkv(t, on)
                if on.hand:
                    t_x1(t)
                if experts:
                    up(m, e + 1)
                if on.hand:
                    lif1(t, q, on)
                if experts:
                    down(m, e)

            def prepare(m, j):
                t = j * PER + PER
                pe.wait_ge(s.x3n_done, t - LAG_G + 1)
                pe.wait_ge(s.in_b, upto(t))
                pe.wait_ge(s.in_c, upto(t - 2))
                router_in(m)

            def finish(m, coming, mixed):
                if mixed:
                    down(m, E - 1)
                if coming is not None:
                    t = (coming - B + 1) * PER + PER
                    pe.wait_ge(s.in_a, upto(t + 2))
                    pe.wait_ge(s.g_copied, t - LAG_G + 1)
                    router(coming)

            def experts(m, e):
                up(m, e)
                if e:
                    down(m, e - 1)

            spiking_block(pe, Steps(pe, None), sub, prepare, experts, finish)

        @block.scalar
        def _(act):
            st = Steps(act, s.act_steps)
            activation = nc.scalar.activation

            def silus(m, e):
                for c in range(CHUNKS):
                    act.wait_ge(s.up_ready, m * 4 * E + 4 * e + 2 * c + 1)
                    if not (is_first(m) and e == 0):
                        act.wait_ge(s.gated, m * 2 * E + 2 * e + c - 1)
                    activation(silu[:, c], up_banks[c][0][:, 0:N], ACT.Silu).then_inc(s.silu_done, 1)

            def router_hi(m):
                act.wait_ge(s.xT_ps, m + 1)
                activation(x_hi[:], side2[:, 0:N], ACT.Copy).then_inc(s.hi_done, 1)

            def top_weights(m):
                act.wait_ge(s.lead_done, m + 1)
                for k in range(TOP):
                    last = activation(top_w[:, k], lead[:], ACT.Sigmoid, scale=1.0 - 2.0 * k)
                last.then_inc(s.top_done, 1)

            def copy_xT(b):
                act.wait_ge(s.xnT_ps, b + 1)
                activation(xnT[:], side0[:, 0:N], ACT.Copy).then_inc(s.xnT_done, 1)

            def copy_qkv(b, tiles):
                if not is_first(b):
                    act.wait_ge(s.qT_ps, b)
                for j in tiles:
                    act.wait_ge(s.qkv_ps, b * TILES + j + 1)
                    ps = (side1, side2)[j % 2]
                    activation(qk[:, j].rearrange("p h d -> p (h d)"), ps[:, 0:2 * C], ACT.Relu)
                    activation(v_one[:, j, 0:C], ps[:, 2 * C:3 * C], ACT.Copy).then_inc(s.qkv_out, 1)

            def copy_qT(b):
                act.wait_ge(s.qT_ps, b + 1)
                activation(qT[:], side1[:, 0:N], ACT.Copy).then_inc(s.qT_done, 1)

            def conv_centre(b):
                act.wait_ge(s.att_done, b + 1)
                activation(conv[:], att[:, 1:N + 1], ACT.Identity, scale=centre_w[:, 0:1],
                           bias=cols[:, DWB:DWB + 1]).then_inc(s.conv_mid, 1)

            act.wait_ge(s.load_c, 16 * LOADS_C)
            activation(half_b1[:], cols[:, B1:B1 + FCH], ACT.Copy, scale=HALF)
            activation(half_b2[:], cols[:, B2:B2 + 1], ACT.Copy, scale=HALF)
            st.did(activation(centre_w[:], cols[:, DW + 1:DW + 2], ACT.Copy, bias=1.0))
            st.settle()
            copy_xT(0)
            copy_qkv(0, range(TILES))
            act.wait_ge(s.load_w, 16 * LOADS_W)
            for e in range(E):
                activation(experts_hi[:, e], experts_f[:, e], ACT.Copy)
            activation(gate_hi[:], gate_f[:], ACT.Copy).then_inc(s.hi_split, 1)
            copy_qT(0)
            conv_centre(0)
            router_hi(0)
            top_weights(0)

            def batch(b, more=True):
                nothing = lambda: None
                side = [lambda: copy_xT(b + 1), lambda: copy_qkv(b + 1, (0, 1)), lambda: copy_qkv(b + 1, (2, 3)),
                        nothing, lambda: copy_qT(b + 1), lambda: conv_centre(b + 1), nothing,
                        lambda: router_hi(b + 1)]
                for e in range(E):
                    silus(b, e)
                    if more:
                        side[e]()
                if more:
                    top_weights(b + 1)

            batch(0)
            with act.Fori(1, B - 1) as b:
                batch(b)
            batch(B - 1, False)

            def fill(t, q, first, n, src, **how):
                if not (isinstance(t, int) and t < 1):
                    act.wait_ge(s.lif_steps, t * 2 * STEPS)
                dst = lif_in[:, (q + 1) % 2, first:first + n].rearrange("p a t -> p (a t)")
                return activation(dst, src, ACT.Identity, scale=HALF, **how)

            def sub(t, q, j, on, experts):
                if experts:
                    m, e = experts
                    silus(m, e)
                if on.fin:
                    act.wait_ge(s.g_ps, t - LAG_G + 1)
                if on.load:
                    act.wait_ge(s.zT_ps, t + 2)
                    activation(zT[:], side0[:, 0:P], ACT.Copy).then_inc(s.zT_done, 1)
                if on.fin:
                    activation(g_tok[:], side0[:, P:2 * P], ACT.Copy).then_inc(s.g_copied, 1)
                if on.ffn:
                    act.wait_ge(s.lif2_ps, t - 2)
                    fill(t, q, CC, B, side2[:, 0:P], bias=half_b2[:, 0:1]).then_inc(s.in_c, 1)
                if on.load:
                    act.wait_ge(s.rkv_ps, t + 2)
                    fill(t, q, CA, 3 * B, side0[:, 0:3 * P]).then_inc(s.in_a, 1)
                if on.hand:
                    act.wait_ge(s.x1T_ps, t)
                    activation(x1T_ring[:, (q - 1) % PER], side1[:, 0:P], ACT.Identity, scale=cols[:, LN1G:LN1G + 1],
                               bias=cols[:, LN1B:LN1B + 1]).then_inc(s.x1T_done, 1)
                if experts:
                    silus(m, e + 1)
                if on.hand:
                    act.wait_ge(s.lif1_ps, t)
                    for k in range(FCH):
                        last = fill(t, q, CB + k * B, B, side2[:, k * P:(k + 1) * P], bias=half_b1[:, k:k + 1])
                    last.then_inc(s.in_b, 1)

            def finish(m, coming, mixed):
                if coming is not None:
                    top_weights(coming)

            spiking_block(act, Steps(act, None), sub, lambda m, j: router_hi(m), silus, finish)

        @block.gpsimd
        def _(pool):
            st = Steps(pool, s.pool_steps)
            g = nc.gpsimd
            g.memset(minus_half[:], -0.5)
            g.memset(v_one[:, :, C:C + 1], 1.0)
            g.memset(att[:, 0:1], 0.0)
            g.memset(att[:, N + 1:N + 2], 0.0)
            g.memset(lif_in[:], 0.0)
            g.memset(lif_v[:], 0.0)
            g.memset(h_decay[:], DECAY)
            st.did(g.memset(h_out[:], 0.0))
            st.settle()
            g.memset(h_decay[:, :, 0:1], 0.0).then_inc(s.zeros, 1)

            def rstd(ln, k):
                wait_apart(pool, ln.has_var, k + 1)
                st.did(g.tensor_scalar(ln.var[:], ln.mv[:, :, 1], LN_EPS, None, ALU.add))
                st.settle()
                n = ln.var.shape[1]
                g.tensor_tensor(ln.rstd[:], ln.var[:], minus_half[:, 0:n], ALU.pow).then_inc(ln.has_rstd, 1)

            def start_sum(m, phase1):
                if phase1:
                    pool.wait_ge(s.res_done, m + 1)
                else:
                    pool.wait_ge(s.x3_done, (m - B + 1) * PER)
                if not is_first(m):
                    wait_apart(pool, s.added, m * (E + 1))
                g.tensor_copy(acc[:], res[:]).then_inc(s.added, 1)

            def add(m, e, phase1):
                pool.wait_ge(s.y_weighted, m * E + e + 1)
                pool.wait_ge(s.added, m * (E + 1) + 1 + e)
                last = e == E - 1
                if last:
                    if phase1 and not is_first(m):
                        pool.wait_ge(s.x2_stored, 16 * m)
                        pool.wait_ge(s.z_done, m)
                    elif not phase1 and isinstance(m, int) and m == B:
                        pool.wait_ge(s.x2_stored, 16 * B)
                        pool.wait_ge(s.z_done, B)
                    elif not phase1:
                        pool.wait_ge(s.out_stored, (m - B) * 16 * PER)
                g.tensor_tensor((moe_out if last else acc)[:], acc[:], weighted[:, e % 2], ALU.add)\
                 .then_inc(s.added, 1)

            def add_bias(b):
                pool.wait_ge(s.x_loaded, 16 * (b + 1))
                if not is_first(b):
                    pool.wait_ge(s.res_done, b)
                for j in range(TILES):
                    last = g.tensor_tensor(x_plus_b[:, j], x_tok[:, j], proj_b[:], ALU.add)
                last.then_inc(s.xb_done, 1)

            def cube(b):
                pool.wait_ge(s.qk_first, b + 1)
                st.did(g.tensor_tensor(qk2[:], qk[:], qk[:], ALU.mult))
                st.settle()
                g.tensor_tensor(qk2[:], qk2[:], qk[:], ALU.mult).then_inc(s.cubed, 1)

            pool.wait_ge(s.load_c, 16 * LOADS_C)
            rstd(ln_x, 0)
            add_bias(0)
            cube(0)
            rstd(ln_r, 0)

            def batch(b, more=True):
                nothing = lambda: None
                side = [lambda: (rstd(ln_x, b + 1), add_bias(b + 1)), nothing, nothing, lambda: cube(b + 1),
                        nothing, nothing, lambda: rstd(ln_r, b + 1), nothing]
                start_sum(b, True)
                for e in range(E):
                    if e:
                        add(b, e - 1, True)
                    if more:
                        side[e]()
                add(b, E - 1, True)
                rstd(ln_z, b)

            rounds(pool, st, 0, B - 1, batch)
            batch(B - 1, False)

            def sub(t, q, j, on, experts):
                if experts:
                    m, e = experts
                    if e == 0:
                        start_sum(m, False)
                if on.fin:
                    c = t - LAG_G
                    place = (q - LAG_G) % PER
                    rstd(ln_g, c)
                if on.hand:
                    rstd(ln_a, t - 1)
                if on.fin:
                    pool.wait_ge(s.g_normed, c + 1)
                    st.did(g.tensor_tensor(g_s[:], g_n[:], ln2_g[:], ALU.mult))
                    st.settle()
                    st.did(g.tensor_tensor(g_s[:], g_s[:], ln2_b[:], ALU.add))
                    st.settle()
                    pool.wait_ge(x2_loaded[place], 16 * j)
                    g.tensor_tensor(res[:, place], g_s[:], x2_ring[:, place], ALU.add).then_inc(s.x3_done, 1)
                if experts and e:
                    add(m, e - 1, False)
                if on.fin:
                    rstd(ln_m, c)
                if experts:
                    add(m, e, False)

            def sums(m, e):
                if e == 0:
                    start_sum(m, False)
                else:
                    add(m, e - 1, False)

            def finish(m, coming, mixed):
                if mixed:
                    add(m, E - 1, False)

            spiking_block(pool, st, sub, lambda m, j: None, sums, finish)

        @block.vector
        def _(dve):
            st = Steps(dve, s.dve_steps)
            v = nc.vector

            def gate_products(m, e):
                for c in range(CHUNKS):
                    dve.wait_ge(s.silu_done, m * 2 * E + 2 * e + c + 1)
                    dve.wait_ge(s.up_ready, m * 4 * E + 4 * e + 2 * c + 2)
                    v.tensor_tensor(hidden[:, e % 2, c], silu[:, c], up_banks[c][1][:, 0:N], ALU.mult)\
                     .then_inc(s.gated, 1)

            def weigh(m, e):
                dve.wait_ge(s.down_ready, m * E + e + 1)
                if not (is_first(m) and e < 2):
                    dve.wait_ge(s.added, m * (E + 1) + (e - 1 if e < 2 else e))
                if e == 0:
                    dve.wait_ge(s.comb_done, m + 1)
                v.tensor_tensor(weighted[:, e % 2], down_bank[:, 0:N].rearrange("p (j c) -> p j c", c=C),
                                comb[:, :, e:e + 1].to_broadcast([P, TILES, C]), ALU.mult).then_inc(s.y_weighted, 1)

            def stats(ln, src, n):
                for j in range(n):
                    ins = v.bn_stats(ln.stats[:, j], src(j))
                st.did(ins)
                st.settle(wait_apart)
                for j in range(n):
                    ins = v.bn_aggr(ln.mv[:, j], ln.stats[:, j])
                ins.then_inc(ln.has_var, 1)

            def normalise(ln, k, dst, src, n, done):
                dve.wait_ge(ln.has_rstd, k + 1)
                for j in range(n):
                    ins = v.tensor_scalar(dst(j), src(j), ln.mv[:, j, 0:1], ln.rstd[:, j:j + 1],
                                          ALU.subtract, ALU.mult)
                ins.then_inc(done, 1)

            def router_lo(m):
                dve.wait_ge(s.hi_done, m + 1)
                v.tensor_tensor(x_lo[:], side2[:, 0:N], x_hi[:].bitcast(fp32), ALU.subtract).then_inc(s.lo_done, 1)

            def route(m):
                dve.wait_ge(s.router_ps, m + 1)
                st.did(v.tensor_copy(scores[:].rearrange("p j e -> p (j e)"), side0[:, 0:TILES * E]))
                st.settle(wait_apart)
                for j in range(TILES):
                    ins = v.max(best[:, j], scores[:, j])
                st.did(ins)
                st.settle()
                v.tensor_tensor(lead[:], best[:, :, 0], best[:, :, 1], ALU.subtract).then_inc(s.lead_done, 1)
                for j in range(TILES):
                    ins = v.max_index(best_no[:, j], best[:, j], scores[:, j])
                st.did(ins)
                st.settle()
                st.did(v.tensor_copy(best_nof[:], best_no[:, :, 0:TOP]))
                st.settle()
                for k in range(TOP):
                    ins = v.tensor_tensor(pick[:, k], expert_no[:].unsqueeze(1).to_broadcast([P, TILES, E]),
                                          best_nof[:, :, k:k + 1].to_broadcast([P, TILES, E]), ALU.is_equal)
                st.did(ins)
                dve.wait_ge(s.top_done, m + 1)
                st.settle()
                for k in range(TOP):
                    ins = v.tensor_tensor(pick[:, k], pick[:, k],
                                          top_w[:, k].unsqueeze(2).to_broadcast([P, TILES, E]), ALU.mult)
                st.did(ins)
                st.settle()
                v.tensor_tensor(comb[:], pick[:, 0], pick[:, 1], ALU.add).then_inc(s.comb_done, 1)

            def norm_x(b):
                dve.wait_ge(s.x_loaded, 16 * (b + 1))
                stats(ln_x, lambda j: x_tok[:, j], TILES)

            def norm_x2(b):
                if not is_first(b):
                    dve.wait_ge(s.xnT_ps, b)
                normalise(ln_x, b, lambda j: xn[:, j], lambda j: x_tok[:, j], TILES, s.xn_done)

            def sums(src):
                st.did(v.tensor_reduce(qk_sum[:], src, axis=AX, op=ALU.add))
                st.settle()
                st.did(v.reciprocal(qk_inv[:], qk_sum[:]))
                st.settle()

            def by_head(t):
                return t[:].unsqueeze(3).to_broadcast([P, TILES, 2 * HEADS, HD])

            def flat(t):
                return t[:].rearrange("p j h d -> p (j h d)")

            def qk_norm1(b):
                dve.wait_ge(s.qkv_out, (b + 1) * TILES)
                st.did(v.tensor_scalar(flat(qk), flat(qk), ATT_EPS, None, ALU.add))
                st.settle()
                sums(qk[:])
                v.tensor_tensor(merge(qk), merge(qk), inv(), ALU.mult).then_inc(s.qk_first, 1)

            def merge(t):
                return t[:].rearrange("p j h d -> p (j h) d")

            def inv():
                return qk_inv[:].rearrange("p j h -> p (j h)").unsqueeze(2).to_broadcast([P, TILES * 2 * HEADS, HD])

            def qk_norm2(b):
                dve.wait_ge(s.cubed, b + 1)
                sums(qk2[:])
                v.tensor_tensor(merge(qk), merge(qk2), inv(), ALU.mult).then_inc(s.qk_done, 1)

            def mask_kv(b):
                dve.wait_ge(s.kv_ps, b + 1)
                if not is_first(b):
                    dve.wait_ge(s.att_ps, b)
                v.tensor_tensor(kv_m[:], side0[:, 0:C], head_mask[:], ALU.mult)
                v.tensor_scalar(ks_m[:], head_mask[:], side0[:, C:C + 1], None, ALU.mult).then_inc(s.kv_masked, 1)

            def attended(b):
                dve.wait_ge(s.att_ps, b + 1)
                st.did(v.tensor_scalar(z_inv[:], side0[:, 0:N], ATT_EPS, None, ALU.add))
                st.settle()
                st.did(v.reciprocal(z_inv[:], z_inv[:]))
                st.settle()
                v.tensor_tensor(att[:, 1:N + 1], side2[:, 0:N], z_inv[:], ALU.mult).then_inc(s.att_done, 1)

            def conv_sides(b):
                dve.wait_ge(s.conv_mid, b + 1)
                dve.wait_ge(s.att_done, b + 1)
                st.did(v.scalar_tensor_tensor(conv[:], att[:, 0:N], cols[:, DW:DW + 1], conv[:], ALU.mult, ALU.add))
                st.settle()
                v.scalar_tensor_tensor(conv[:], att[:, 2:N + 2], cols[:, DW + 2:DW + 3], conv[:], ALU.mult, ALU.add)\
                 .then_inc(s.conv_done, 1)

            def residual(b):
                dve.wait_ge(s.proj_ps, b + 1)
                dve.wait_ge(s.xb_done, b + 1)
                if not is_first(b):
                    dve.wait_ge(s.added, (b - 1) * (E + 1) + 1)
                v.tensor_tensor(res[:].rearrange("p j c -> p (j c)"), side1[:, 0:N],
                                x_plus_b[:].rearrange("p j c -> p (j c)"), ALU.add).then_inc(s.res_done, 1)
                dve.wait_ge(s.res_done, b + 1)
                stats(ln_r, lambda j: res[:, j], TILES)

            def norm_res(b):
                if not is_first(b):
                    dve.wait_ge(s.xT_ps, b)
                normalise(ln_r, b, lambda j: resn[:, j], lambda j: res[:, j], TILES, s.resn_done)

            def norm_out(b):
                dve.wait_ge(s.added, b * (E + 1) + E + 1)
                stats(ln_z, lambda j: moe_out[:, j], TILES)
                if not is_first(b):
                    dve.wait_ge(s.z_stored, 16 * b)
                normalise(ln_z, b, lambda j: z_tok[:, j], lambda j: moe_out[:, j], TILES, s.z_done)

            dve.wait_ge(s.zeros, 1)
            dve.wait_ge(s.load_c, 16 * LOADS_C)
            norm_x(0)
            norm_x2(0)
            qk_norm1(0)
            qk_norm2(0)
            mask_kv(0)
            attended(0)
            conv_sides(0)
            dve.wait_ge(s.hi_split, 1)
            v.tensor_tensor(experts_lo[:], experts_f[:], experts_hi[:].bitcast(fp32), ALU.subtract)
            v.tensor_tensor(gate_lo[:], gate_f[:], gate_hi[:].bitcast(fp32), ALU.subtract).then_inc(s.lo_split, 1)
            st.did(v.tensor_copy(lif2_part[:, 0], lif2_f[:]))
            st.settle()
            st.did(v.tensor_tensor(lif2_rest[:], lif2_f[:], lif2_part[:, 0], ALU.subtract))
            st.settle()
            st.did(v.tensor_copy(lif2_part[:, 1], lif2_rest[:]))
            st.settle()
            st.did(v.tensor_tensor(lif2_rest[:], lif2_rest[:], lif2_part[:, 1], ALU.subtract))
            st.settle()
            v.tensor_copy(lif2_part[:, 2], lif2_rest[:]).then_inc(s.lo_split, 1)
            residual(0)
            norm_res(0)
            router_lo(0)
            route(0)

            def batch(b, more=True):
                nothing = lambda: None
                side = [lambda: norm_x(b + 1), lambda: norm_x2(b + 1), nothing, lambda: qk_norm1(b + 1),
                        lambda: (qk_norm2(b + 1), mask_kv(b + 1)), lambda: (attended(b + 1), conv_sides(b + 1)),
                        lambda: residual(b + 1), lambda: (norm_res(b + 1), router_lo(b + 1))]
                pre = [lambda: norm_x2(b + 1)] + [nothing] * 7
                for e in range(E):
                    if more and e == 0:
                        norm_x(b + 1)
                    gate_products(b, e)
                    if more and e == 0:
                        norm_x2(b + 1)
                    if e:
                        weigh(b, e - 1)
                    if more and e >= 2:
                        side[e]()
                weigh(b, E - 1)
                if more:
                    route(b + 1)
                norm_out(b)

            rounds(dve, st, 0, B - 1, batch)
            batch(B - 1, False)

            def sub(t, q, j, on, experts):
                if not on.scan and not on.fin:
                    return
                now, old = lif_u[:, q % 2], lif_u[:, (q + 1) % 2]
                source = lif_in[:, q % 2]
                if experts:
                    m, e = experts

                def carry_in():
                    v.tensor_copy(kv_in[:, :, 0:1], h_out[:, :, STEPS:STEPS + 1])
                    st.did(v.tensor_scalar(v_spike[:], old[:, 2 * B:3 * B], V_TH, None, ALU.is_ge))

                def spikes_kv():
                    st.settle()
                    st.did(v.scalar_tensor_tensor(kv_in[:, :, 1:], old[:, B:2 * B], V_TH, v_spike[:],
                                                  ALU.is_ge, ALU.mult))

                def scan_h():
                    st.settle()
                    st.did(v.tensor_tensor_scan(h_out[:].rearrange("p b t -> p (b t)"),
                                                h_decay[:].rearrange("p b t -> p (b t)"),
                                                kv_in[:].rearrange("p b t -> p (b t)"), 0.0, ALU.mult, ALU.add))

                def gate_h():
                    st.settle()
                    if not (isinstance(t, int) and t < 2):
                        dve.wait_ge(s.wo_ps, t - 1)
                    v.scalar_tensor_tensor(y_fm[:].rearrange("p (b t) -> p b t", b=B), old[:, 0:B], V_TH,
                                           h_out[:, :, 1:], ALU.is_ge, ALU.mult).then_inc(s.y_done, 1)

                def ffn_spikes():
                    if not (isinstance(t, int) and t < 4):
                        dve.wait_ge(s.lif2_ps, t - 3)
                    v.tensor_scalar(s1[:].rearrange("p k t -> p (k t)"),
                                    old[:, CB:CB + FCH * B].rearrange("p a t -> p (a t)"), V_TH, None, ALU.is_ge)\
                     .then_inc(s.s1_done, 1)

                def final_sum():
                    if not (isinstance(t, int) and t < LAG_G + 1):
                        dve.wait_ge(s.g_ps, t - LAG_G)
                    v.scalar_tensor_tensor(gT[:], old[:, CC:CC + B].rearrange("p a t -> p (a t)"), V_TH,
                                           x1T_ring[:, (q - LAG_G) % PER], ALU.is_ge, ALU.add).then_inc(s.g_done, 1)

                def x1_sum():
                    dve.wait_ge(s.wo_ps, t)
                    v.tensor_tensor(x1p[:], side1[:, 0:C], z_ring[:, (q - 1) % PER], ALU.add).then_inc(s.x1p_done, 1)

                def x1_stats():
                    dve.wait_ge(s.x1p_done, t)
                    st.did(v.bn_stats(ln_a.stats[:, 0], x1p[:]))

                def x1_aggr():
                    st.settle(wait_apart)
                    v.bn_aggr(ln_a.mv[:, 0], ln_a.stats[:, 0]).then_inc(ln_a.has_var, 1)

                def x1_norm():
                    normalise(ln_a, t - 1, lambda j: x1n[:], lambda j: x1p[:], 1, s.x1n_done)

                def g_stats():
                    dve.wait_ge(s.g_copied, t - LAG_G + 1)
                    st.did(v.bn_stats(ln_g.stats[:, 0], g_tok[:]))

                def g_aggr():
                    st.settle(wait_apart)
                    v.bn_aggr(ln_g.mv[:, 0], ln_g.stats[:, 0]).then_inc(ln_g.has_var, 1)

                def g_norm():
                    normalise(ln_g, t - LAG_G, lambda j: g_n[:], lambda j: g_tok[:], 1, s.g_normed)

                def m_stats():
                    dve.wait_ge(s.x3_done, t - LAG_G + 1)
                    st.did(v.bn_stats(ln_m.stats[:, 0], res[:, (q - LAG_G) % PER]))

                def m_aggr():
                    st.settle(wait_apart)
                    v.bn_aggr(ln_m.mv[:, 0], ln_m.stats[:, 0]).then_inc(ln_m.has_var, 1)

                def m_norm():
                    place = (q - LAG_G) % PER
                    normalise(ln_m, t - LAG_G, lambda j: resn[:, place], lambda j: res[:, place], 1, s.x3n_done)

                fill = []

                def at(slot, *ops):
                    fill.append((slot, ops))

                if on.fin:
                    at(0, final_sum)
                if on.hand:
                    at(1, carry_in)
                    at(2, spikes_kv)
                    at(3, scan_h)
                    at(4, gate_h)
                if on.ffn:
                    at(5, ffn_spikes)
                if on.fin:
                    at(6, g_stats)
                    at(7, g_aggr)
                if on.hand:
                    at(8, x1_sum)
                    at(9, x1_stats)
                    at(10, x1_aggr)
                if experts:
                    at(11, lambda: gate_products(m, e))
                if on.fin:
                    at(12, g_norm)
                if on.hand:
                    at(13, x1_norm)
                if experts and e:
                    at(16, lambda: weigh(m, e - 1))
                if on.fin:
                    at(20, m_stats)
                    at(21, m_aggr)
                if experts:
                    at(23, lambda: gate_products(m, e + 1))
                if on.fin:
                    at(25, m_norm)
                if experts:
                    at(29, lambda: weigh(m, e))

                def side(slot):
                    for when, ops in fill:
                        if when == slot:
                            for op in ops:
                                op()

                if on.load or on.hand:
                    dve.wait_ge(s.in_a, upto(t + 1))
                if not (isinstance(t, int) and t < 2):
                    dve.wait_ge(s.in_b, upto(t - 1))
                if not (isinstance(t, int) and t < 4):
                    dve.wait_ge(s.in_c, upto(t - 3))
                for i in range(STEPS):
                    if on.scan:
                        if not (i == 0 and is_first(t)):
                            dve.wait_ge(s.lif_steps, t * 2 * STEPS + 2 * i)
                        v.scalar_tensor_tensor(now[:, :, i], lif_v[:], HALF, source[:, :, i], ALU.mult, ALU.add)\
                         .then_inc(s.lif_steps, 1)
                    side(2 * i)
                    if on.scan:
                        dve.wait_ge(s.lif_steps, t * 2 * STEPS + 2 * i + 1)
                        v.scalar_tensor_tensor(lif_v[:], now[:, :, i], V_TH, now[:, :, i], ALU.is_lt, ALU.mult)\
                         .then_inc(s.lif_steps, 1)
                    side(2 * i + 1)

            def experts_alone(m, e):
                gate_products(m, e)
                if e:
                    weigh(m, e - 1)

            def finish(m, coming, mixed):
                if mixed:
                    weigh(m, E - 1)
                if coming is not None:
                    route(coming)

            spiking_block(dve, st, sub, lambda m, j: router_lo(m), experts_alone, finish)

    return nc


def kernel(**inputs):
    import numpy as np
    import concourse.bacc as bacc
    from concourse.bass_utils import run_bass_kernel_spmd

    a, b, f = "L0_attn_a_", "L0_attn_b_", "L0_ffn_"
    given = {k: np.asarray(v) for k, v in inputs.items()}
    p = np.arange(128)

    def columns(v):
        return v.reshape(-1, 128).T

    arrays = {
        "x": given[a + "x"],
        "qkv_w": given[a + "w_qkv"].T,
        "proj_w": given[a + "w_proj"].T,
        "b_proj": given[a + "b_proj"],
        "wr": given[b + "Wr"].T,
        "wk": given[b + "Wk"].T,
        "wv": given[b + "Wv"].T,
        "wo": given[b + "Wo"].T,
        "lif_w1": given[b + "W1"].T,
        "lif_w2": given[b + "W2"].T,
        "ln2_g": given[b + "ln2_g"],
        "ln2_b": given[b + "ln2_b"],
        "Wg": given[f + "Wg"],
        "W1": given[f + "W1"],
        "W3": given[f + "W3"],
        "W2": given[f + "W2"],
        "cols": np.concatenate([columns(given[b + "b1"]), columns(given[b + "b2"]), columns(given[b + "ln1_g"]),
                                columns(given[b + "ln1_b"]), given[a + "w_dwc"], columns(given[a + "b_dwc"])],
                               axis=1),
        "ident": np.eye(128, dtype=np.float32),
        "head_mask": (p[:, None] // 8 == p[None, :] // 8).astype(np.float32),
        "expert_no": np.tile(np.arange(8, dtype=np.float32), (128, 1)),
    }
    arrays = {k: np.ascontiguousarray(v) for k, v in arrays.items()}
    nc = bacc.Bacc("TRN2", target_bir_lowering=False, num_devices=1)
    dram, feeds = {}, {}
    for name, value in arrays.items():
        dram[name] = nc.dram_tensor(f"in_{name}", value.shape, mybir.dt.from_np(value.dtype),
                                    kind="ExternalInput").ap()
        feeds[f"in_{name}"] = value
    dram["out"] = nc.dram_tensor("out_x", arrays["x"].shape, mybir.dt.float32, kind="ExternalOutput").ap()
    build_program(nc, dram)
    done = run_bass_kernel_spmd(nc, [feeds], core_ids=[0])
    return done.results[0]["out_x"]
```

```python
import concourse.bass as bass
from concourse import mybir
from contextlib import ExitStack
from collections import namedtuple


LayerNorm = namedtuple("LayerNorm", "stats mv var rstd has_var has_rstd")
Stages = namedtuple("Stages", "load hand ffn fin scan")


class Steps:

    def __init__(self, eng, sem):
        self.eng, self.sem, self.n, self.base = eng, sem, 0, 0

    def did(self, instruction):
        instruction.then_inc(self.sem, 1)
        self.n += 1

    def settle(self, wait=None):
        if wait:
            wait(self.eng, self.sem, self.base + self.n)
        else:
            self.eng.wait_ge(self.sem, self.base + self.n)


def rounds(eng, steps, start, end, body, each=0):
    before = steps.n
    with eng.Fori(start, end) as i:
        steps.base = (i - start) * each
        body(i)
    assert steps.n == before + each, steps.n - before
    steps.n, steps.base = before + (end - start) * each, 0


def peeled(eng, steps, start, end, body):
    before = steps.n
    body(start)
    rounds(eng, steps, start + 1, end, body, steps.n - before)


def is_first(i):
    return isinstance(i, int) and i == 0


def build_program(nc, dram):
    fp32 = mybir.dt.float32
    fp32r = mybir.dt.float32r
    bf16 = mybir.dt.bfloat16
    u32 = mybir.dt.uint32
    ALU = mybir.AluOpType
    ACT = mybir.ActivationFunctionType
    AX = mybir.AxisListType.X

    x_in_dram, out_dram = dram["x"], dram["out"]
    B, N, C = x_in_dram.shape
    P = 128
    TILES = N // P
    E, _, HID = dram["W1"].shape
    CHUNKS = HID // P
    F = dram["lif_w1"].shape[1]
    FCH = F // P
    HEADS, HD = 16, 8
    TOP = 2
    LN_EPS, ATT_EPS = 1e-5, 1e-6
    V_TH, DECAY, HALF = 1.0, 0.9, 0.5
    STEPS = P // B
    SUBS = N // STEPS
    PER = 4
    COLS = (3 + FCH + 1) * B
    CA, CB, CC = 0, 3 * B, (3 + FCH) * B
    LAG_B, LAG_C, LAG_G = 2, 4, 5

    ctx = ExitStack()
    with ctx:
        def sb(name, shape, dt=fp32):
            return ctx.enter_context(nc.sbuf_tensor(name, shape, dt))

        def sem(name):
            return ctx.enter_context(nc.semaphore(name))

        experts_f = sb("experts_f", [P, E, 2 * HID])
        experts_hi = sb("experts_hi", [P, E, 2 * HID], fp32r)
        experts_lo = sb("experts_lo", [P, E, 2 * HID], fp32r)
        down_w = sb("down_w", [P, E, CHUNKS, C])
        gate_f = sb("gate_f", [P, E])
        gate_hi = sb("gate_hi", [P, E], fp32r)
        gate_lo = sb("gate_lo", [P, E], fp32r)
        qkv_w = sb("qkv_w", [P, 3 * C])
        proj_w = sb("proj_w", [P, C])
        rkv_w = sb("rkv_w", [P, 3, C])
        wo_w = sb("wo_w", [P, C])
        lif1_w = sb("lif1_w", [P, F])
        lif2_f = sb("lif2_f", [P, FCH, C])
        lif2_rest = sb("lif2_rest", [P, FCH, C])
        lif2_part = sb("lif2_part", [P, 3, FCH, C], bf16)
        ident = sb("ident", [P, P])
        head_mask = sb("head_mask", [P, P])
        expert_no = sb("expert_no", [P, E])
        cols = sb("cols", [P, FCH + 7])
        half_b1 = sb("half_b1", [P, FCH])
        half_b2 = sb("half_b2", [P, 1])
        centre_w = sb("centre_w", [P, 1])
        proj_b = sb("proj_b", [P, C])
        ln2_g = sb("ln2_g", [P, C])
        ln2_b = sb("ln2_b", [P, C])
        minus_half = sb("minus_half", [P, TILES])
        B1, B2, LN1G, LN1B, DW, DWB = 0, FCH, FCH + 1, FCH + 2, FCH + 3, FCH + 6

        res = sb("res", [P, TILES, C])
        resn = sb("resn", [P, TILES, C])
        x_hi = sb("x_hi", [P, N], fp32r)
        x_lo = sb("x_lo", [P, N], fp32r)
        silu = sb("silu", [P, CHUNKS, N])
        hidden = sb("hidden", [P, 2, CHUNKS, N])
        weighted = sb("weighted", [P, 2, TILES, C])
        acc = sb("acc", [P, TILES, C])
        moe_out = sb("moe_out", [P, TILES, C])
        scores = sb("scores", [P, TILES, E])
        best = sb("best", [P, TILES, 8])
        best_no = sb("best_no", [P, TILES, 8], u32)
        best_nof = sb("best_nof", [P, TILES, TOP])
        lead = sb("lead", [P, TILES])
        lead_tanh = sb("lead_tanh", [P, TILES])
        top_w = sb("top_w", [P, TOP, TILES])
        pick = sb("pick", [P, TOP, TILES, E])
        comb = sb("comb", [P, TILES, E])

        def ln_set(name, n):
            return LayerNorm(stats=sb(name + "_stats", [P, n, 6]), mv=sb(name + "_mv", [P, n, 2]),
                             var=sb(name + "_var", [P, n]), rstd=sb(name + "_rstd", [P, n]),
                             has_var=sem(name + "_has_var"), has_rstd=sem(name + "_has_rstd"))

        ln_x = ln_set("ln_x", TILES)
        ln_r = ln_set("ln_r", TILES)
        ln_z = ln_set("ln_z", TILES)
        ln_a = ln_set("ln_a", 1)
        ln_g = ln_set("ln_g", 1)
        ln_m = ln_set("ln_m", 1)

        x_tok = sb("x_tok", [P, TILES, C])
        x_plus_b = sb("x_plus_b", [P, TILES, C])
        xn = sb("xn", [P, TILES, C])
        xnT = sb("xnT", [P, N])
        qk = sb("qk", [P, TILES, 2 * HEADS, HD])
        qk2 = sb("qk2", [P, TILES, 2 * HEADS, HD])
        qk_sum = sb("qk_sum", [P, TILES, 2 * HEADS])
        qk_inv = sb("qk_inv", [P, TILES, 2 * HEADS])
        v_one = sb("v_one", [P, TILES, C + 1])
        kv_m = sb("kv_m", [P, C])
        ks_m = sb("ks_m", [P, C])
        qT = sb("qT", [P, N])
        z_inv = sb("z_inv", [P, N])
        att = sb("att", [P, N + 2])
        conv = sb("conv", [P, N])
        z_tok = sb("z_tok", [P, TILES, C])

        lif_in = sb("lif_in", [P, 2, COLS, STEPS])
        lif_u = sb("lif_u", [P, 2, COLS, STEPS])
        lif_v = sb("lif_v", [P, COLS])
        z_ring = sb("z_ring", [P, PER, C])
        x2_ring = sb("x2_ring", [P, PER, C])
        x1T_ring = sb("x1T_ring", [P, PER, P])
        zT = sb("zT", [P, P])
        v_spike = sb("v_spike", [P, B, STEPS])
        kv_in = sb("kv_in", [P, B, STEPS + 1])
        h_out = sb("h_out", [P, B, STEPS + 1])
        h_decay = sb("h_decay", [P, B, STEPS + 1])
        y_fm = sb("y_fm", [P, P])
        x1p = sb("x1p", [P, C])
        x1n = sb("x1n", [P, C])
        s1 = sb("s1", [P, FCH, P], bf16)
        gT = sb("gT", [P, P])
        g_tok = sb("g_tok", [P, C])
        g_n = sb("g_n", [P, C])
        g_s = sb("g_s", [P, C])

        def bank(name):
            return ctx.enter_context(nc.psum_tensor(name, [P, 512], fp32))

        up_banks = [[bank("up_a1"), bank("up_a3")], [bank("up_b1"), bank("up_b3")]]
        down_bank = bank("down_bank")
        side0, side1, side2 = bank("side0"), bank("side1"), bank("side2")

        signals = """
            load_w load_c x_loaded zeros hi_split lo_split
            up_ready silu_done gated down_ready y_weighted added
            xT_ps hi_done lo_done router_ps scores_done lead_done tanh_done top_done comb_done
            xn_done xnT_ps xnT_done qkv_ps qkv_out qk_first cubed cubes_summed cubes_inverse qk_done kv_ps kv_masked qT_ps qT_done
            att_ps z_added z_inverse att_done conv_mid conv_done proj_ps xb_done res_done resn_done
            z_done x2_stored z_stored
            zT_ps zT_done rkv_ps in_a y_done wo_ps x1p_done x1n_done x1T_ps x1T_done lif1_ps in_b
            s1_done lif2_ps in_c g_done g_ps g_copied g_normed x3_done x3n_done
            lif_steps dve_steps act_steps pool_steps out_stored""".split()
        s = namedtuple("Signals", signals)(*[sem(n) for n in signals])

        z_loaded = [sem(f"z_loaded{q}") for q in range(PER)]
        x2_loaded = [sem(f"x2_loaded{q}") for q in range(PER)]

        x2_dram = nc.dram_tensor("x2_scratch", (B, N, C), fp32, kind="Internal").ap()
        z_dram = nc.dram_tensor("z_scratch", (B, N, C), fp32, kind="Internal").ap()

        def rows_of_batch(t, b):
            return t[bass.ds(b, 1)].rearrange("o (j p) c -> p (o j) c", p=P)

        block = ctx.enter_context(nc.Block())
        LOADS_W, LOADS_C = 11, 8
        GROUPS = SUBS // PER


        def wait_apart(eng, which, count):
            if not isinstance(count, int):
                count = eng.to_reg(count)
                eng.wait_ge(s.zeros, 1)
            eng.wait_ge(which, count)

        def first_half(lead_in, slot, end, expert, closing, rest, loop):
            for a, c in ((0, None), (1, 0)):
                for k in range(E):
                    slot(k, a, c)
                    if c == 0:
                        lead_in(k)
                end(a, c, lambda: None)

            def batch(b):
                known = isinstance(b, int)
                a = None if known and b + 2 >= B else b + 2
                c = None if known and b + 1 >= B else b + 1
                for e in range(E):
                    expert(b, e, lambda: slot(e, a, c))
                    rest(b, e)
                end(a, c, lambda: closing(b))

            batch(0)
            loop(1, B - 2, batch)
            batch(B - 2)
            batch(B - 1)

        def stages(t):
            if not isinstance(t, int):
                return Stages(load=True, hand=True, ffn=True, fin=True, scan=True)
            return Stages(load=t + 1 < SUBS, hand=0 <= t - 1 < SUBS, ffn=0 <= t - 3 < SUBS,
                           fin=0 <= t - LAG_G < SUBS, scan=0 <= t < SUBS + LAG_C)

        def upto(n):
            return min(n, SUBS) if isinstance(n, int) else n

        def spiking_block(eng, steps, sub, prepare, experts, finish):
            sub(-1, PER - 1, -1, stages(-1), None)
            sub(0, 0, -1, stages(0), None)

            def group(j, mixed=True, last=False):
                m = B - 2 + j
                for i in range(PER):
                    t = j * PER + 1 + i
                    if last:
                        for e in (2 * i, 2 * i + 1):
                            experts(m, e)
                    else:
                        sub(t, (1 + i) % PER, j, stages(t), (m, 2 * i) if mixed else None)
                prepare(m + 1, j) if not last and not (isinstance(j, int) and j == 0) else None
                finish(m, None if last or (isinstance(j, int) and j == 0) else m + 1, mixed)

            group(0, mixed=False)
            group(1, mixed=False)
            full = (SUBS - 2) // PER
            peeled(eng, steps, 2, full, group)
            for j in range(full, GROUPS + 1):
                group(j)
            group(GROUPS + 1, last=True)

        @block.sync
        def _(sp):
            for dst, src in ((ident[:], dram["ident"]), (head_mask[:], dram["head_mask"]),
                             (expert_no[:], dram["expert_no"]), (cols[:], dram["cols"]),
                             (proj_b[:], dram["b_proj"].partition_broadcast(P)),
                             (ln2_g[:], dram["ln2_g"].partition_broadcast(P)),
                             (ln2_b[:], dram["ln2_b"].partition_broadcast(P)),
                             (qkv_w[:], dram["qkv_w"])):
                sp.dma_start(dst, src).then_inc(s.load_c, 16)

            def load_x(b):
                if not is_first(b):
                    sp.wait_ge(s.xn_done, b)
                    sp.wait_ge(s.xb_done, b)
                sp.dma_start(x_tok[:], rows_of_batch(x_in_dram, b)).then_inc(s.x_loaded, 16)

            load_x(0)
            for dst, src in ((experts_f[:, :, 0:HID], dram["W1"].rearrange("e d h -> d e h")),
                             (experts_f[:, :, HID:], dram["W3"].rearrange("e d h -> d e h")),
                             (down_w[:], dram["W2"].rearrange("e (k p) d -> p e k d", p=P)),
                             (gate_f[:], dram["Wg"]), (proj_w[:], dram["proj_w"]),
                             (rkv_w[:, 0], dram["wr"]), (rkv_w[:, 1], dram["wk"]), (rkv_w[:, 2], dram["wv"]),
                             (wo_w[:], dram["wo"]), (lif1_w[:], dram["lif_w1"]),
                             (lif2_f[:], dram["lif_w2"].rearrange("(k p) d -> p k d", p=P))):
                sp.dma_start(dst, src).then_inc(s.load_w, 16)

            def store_x2(b):
                sp.wait_ge(s.added, b * (E + 1) + E + 1)
                sp.dma_start(rows_of_batch(x2_dram, b), moe_out[:]).then_inc(s.x2_stored, 16)

            def store_z(b):
                sp.wait_ge(s.z_done, b + 1)
                sp.dma_start(rows_of_batch(z_dram, b), z_tok[:]).then_inc(s.z_stored, 16)

            load_x(1)
            load_x(2)

            def batch(b):
                store_x2(b)
                store_z(b)
                load_x(b + 4)

            load_x(3)
            batch(0)
            with sp.Fori(1, B - 4) as b:
                batch(b)
            for b in range(B - 4, B):
                store_x2(b)
                store_z(b)

            sp.wait_ge(s.x2_stored, 16 * B)
            sp.wait_ge(s.z_stored, 16 * B)

            def by_time(t, c):
                return t[:, bass.ds(c * STEPS, STEPS), :]

            def tile(t):
                return t

            def load_z(c, slot):
                if not isinstance(c, int) or c >= PER:
                    sp.wait_ge(s.x1p_done, c - PER + 1)
                sp.dma_start(tile(z_ring[:, slot]), by_time(z_dram, c)).then_inc(z_loaded[slot], 16)

            def load_x2(c, slot):
                if not isinstance(c, int) or c >= PER:
                    sp.wait_ge(s.x3_done, c - PER + 1)
                sp.dma_start(tile(x2_ring[:, slot]), by_time(x2_dram, c)).then_inc(x2_loaded[slot], 16)

            def store_out(k):
                sp.wait_ge(s.added, (B + k) * (E + 1) + E + 1)
                for q in range(PER):
                    sp.dma_start(by_time(out_dram, k * PER + q), tile(moe_out[:, q])).then_inc(s.out_stored, 16)

            for c in range(PER):
                load_z(c, c)
            for c in range(PER):
                load_x2(c, c)

            def group(j):
                if not (isinstance(j, int) and j < 4):
                    store_out(j - 4)
                for q in range(PER):
                    load_z(j * PER + q, q)
                    if not (isinstance(j, int) and j < 2):
                        load_x2((j - 1) * PER + q, q)

            for j in range(1, 4):
                group(j)
            with sp.Fori(4, GROUPS) as j:
                group(j)
            store_out(GROUPS - 4)
            for q in range(PER):
                load_x2((GROUPS - 1) * PER + q, q)
            for k in range(GROUPS - 3, GROUPS):
                store_out(k)
            sp.wait_ge(s.out_stored, 16 * SUBS)

        @block.tensor
        def _(pe):
            mm = nc.tensor.matmul

            def three(out, w_hi, w_lo, m_hi, m_lo):
                mm(out, w_lo, m_hi, start=True, stop=False)
                mm(out, w_hi, m_lo, start=False, stop=False)
                return mm(out, w_hi, m_hi, start=False, stop=True)

            def up(m, e, chunks=range(CHUNKS)):
                for c in chunks:
                    if not (is_first(m) and e == 0):
                        pe.wait_ge(s.gated, m * 2 * E + 2 * e + c - 1)
                    for k in range(2):
                        lo = k * HID + c * P
                        three(up_banks[c][k][:, 0:N], experts_hi[:, e, lo:lo + P], experts_lo[:, e, lo:lo + P],
                              x_hi[:], x_lo[:]).then_inc(s.up_ready, 1)

            def down(m, e):
                pe.wait_ge(s.gated, m * 2 * E + 2 * e + 2)
                if not (is_first(m) and e == 0):
                    pe.wait_ge(s.y_weighted, m * E + e)
                for j in range(TILES):
                    for c in range(CHUNKS):
                        last = mm(down_bank[:, j * C:(j + 1) * C], hidden[:, e % 2, c, j * P:(j + 1) * P],
                                  down_w[:, e, c], start=(c == 0), stop=(c == CHUNKS - 1))
                last.then_inc(s.down_ready, 1)

            def router_in(m):
                for j in range(TILES):
                    last = nc.tensor.transpose(side2[:, j * P:(j + 1) * P], resn[:, j], ident[:])
                last.then_inc(s.xT_ps, 1)

            def router(m):
                pe.wait_ge(s.lo_done, m + 1)
                for j in range(TILES):
                    t = slice(j * P, (j + 1) * P)
                    last = three(side0[:, j * E:(j + 1) * E], x_hi[:, t], x_lo[:, t], gate_hi[:], gate_lo[:])
                last.then_inc(s.router_ps, 1)

            def t_x(b):
                pe.wait_ge(s.xn_done, b + 1)
                if not is_first(b):
                    pe.wait_ge(s.z_added, b)
                for j in range(TILES):
                    last = nc.tensor.transpose(side0[:, j * P:(j + 1) * P], xn[:, j], ident[:])
                last.then_inc(s.xnT_ps, 1)

            def qkv(b, tiles):
                pe.wait_ge(s.xnT_done, b + 1)
                for j in tiles:
                    if j >= 2:
                        pe.wait_ge(s.qkv_out, b * TILES + j - 1)
                    elif j == 1 and not is_first(b):
                        pe.wait_ge(s.att_done, b)
                    mm((side1, side2)[j % 2][:, 0:3 * C], xnT[:, j * P:(j + 1) * P], qkv_w[:],
                       start=True, stop=True).then_inc(s.qkv_ps, 1)

            def kv(b):
                pe.wait_ge(s.qk_done, b + 1)
                for j in range(TILES):
                    k_tile = qk[:, j, HEADS:2 * HEADS].rearrange("p h d -> p (h d)")
                    last = mm(side0[:, 0:C + 1], k_tile, v_one[:, j], start=(j == 0), stop=(j == TILES - 1))
                last.then_inc(s.kv_ps, 1)
                if not is_first(b):
                    pe.wait_ge(s.res_done, b)
                for j in range(TILES):
                    q_tile = qk[:, j, 0:HEADS].rearrange("p h d -> p (h d)")
                    last = nc.tensor.transpose(side1[:, j * P:(j + 1) * P], q_tile, ident[:])
                last.then_inc(s.qT_ps, 1)

            def attend(b):
                pe.wait_ge(s.kv_masked, b + 1)
                pe.wait_ge(s.qT_done, b + 1)
                if not is_first(b):
                    pe.wait_ge(s.scores_done, b)
                mm(side0[:, 0:N], ks_m[:], qT[:], start=True, stop=True)
                mm(side2[:, 0:N], kv_m[:], qT[:], start=True, stop=True).then_inc(s.att_ps, 1)

            def project(b, following):
                pe.wait_ge(s.conv_done, b + 1)
                if following is not None:
                    pe.wait_ge(s.qkv_out, (following + 1) * TILES)
                for j in range(TILES):
                    last = mm(side1[:, j * C:(j + 1) * C], conv[:, j * P:(j + 1) * P], proj_w[:],
                              start=True, stop=True)
                last.then_inc(s.proj_ps, 1)

            def slot(k, a, c):
                if k == 0 and c is not None:
                    attend(c)
                if k == 1 and a is not None:
                    t_x(a)
                if k == 2 and a is not None:
                    qkv(a, (0, 1))
                if k == 3 and a is not None:
                    qkv(a, (2, 3))
                if k == 4 and c is not None:
                    project(c, a)

            def end(a, c, closing):
                if a is not None:
                    kv(a)
                if c is not None:
                    pe.wait_ge(s.resn_done, c + 1)
                    router_in(c)
                closing()
                if c is not None:
                    if a is not None:
                        pe.wait_ge(s.kv_masked, a + 1)
                    router(c)

            def expert(b, e, beside):
                up(b, e)
                if e:
                    down(b, e - 1)
                beside()

            def lead_in(k):
                if k == 3:
                    pe.wait_ge(s.load_w, 16 * LOADS_W)
                if k == E - 1:
                    pe.wait_ge(s.lo_split, 2)

            def loop(start, last, batch):
                with pe.Fori(start, last) as b:
                    batch(b)

            pe.wait_ge(s.load_c, 16 * LOADS_C)
            first_half(lead_in, slot, end, expert, lambda b: down(b, E - 1), lambda b, e: None, loop)

            def t_z(t, q, j):
                place = (q + 1) % PER
                pe.wait_ge(z_loaded[place], 16 * (j + (2 if place in (0, 1) else 1)))
                if not (isinstance(t, int) and t < 0):
                    pe.wait_ge(s.in_a, t + 1)
                nc.tensor.transpose(side0[:, 0:P], z_ring[:, place], ident[:]).then_inc(s.zT_ps, 1)

            def t_g(t):
                pe.wait_ge(s.g_done, t - LAG_G + 1)
                if not (isinstance(t, int) and t < LAG_G + 1):
                    pe.wait_ge(s.g_copied, t - LAG_G)
                nc.tensor.transpose(side0[:, P:2 * P], gT[:], ident[:]).then_inc(s.g_ps, 1)

            def rkv(t, on):
                pe.wait_ge(s.zT_done, t + 2)
                if on.fin:
                    pe.wait_ge(s.g_copied, t - LAG_G + 1)
                for k in range(3):
                    last = mm(side0[:, k * P:(k + 1) * P], rkv_w[:, k], zT[:], start=True, stop=True)
                last.then_inc(s.rkv_ps, 1)

            def wo(t):
                pe.wait_ge(s.y_done, t)
                if not (isinstance(t, int) and t < 2):
                    pe.wait_ge(s.x1T_done, t - 1)
                mm(side1[:, 0:C], y_fm[:], wo_w[:], start=True, stop=True).then_inc(s.wo_ps, 1)

            def t_x1(t):
                pe.wait_ge(s.x1n_done, t)
                nc.tensor.transpose(side1[:, 0:P], x1n[:], ident[:]).then_inc(s.x1T_ps, 1)

            def lif1(t, q, on):
                pe.wait_ge(s.x1T_done, t)
                if on.ffn:
                    pe.wait_ge(s.in_c, t - 2)
                elif t > 1:
                    pe.wait_ge(s.in_b, t - 1)
                for k in range(FCH):
                    last = mm(side2[:, k * P:(k + 1) * P], lif1_w[:, k * P:(k + 1) * P], x1T_ring[:, (q - 1) % PER],
                              start=True, stop=True)
                last.then_inc(s.lif1_ps, 1)

            def lif2(t):
                pe.wait_ge(s.s1_done, t - 2)
                pe.wait_ge(s.in_b, upto(t - 1))
                if not (isinstance(t, int) and t < 4):
                    pe.wait_ge(s.in_c, t - 3)
                for k in range(FCH):
                    for part in range(3):
                        last = mm(side2[:, 0:P], lif2_part[:, 2 - part, k], s1[:, k],
                                  start=(k == 0 and part == 0), stop=(k == FCH - 1 and part == 2))
                last.then_inc(s.lif2_ps, 1)

            def sub(t, q, j, on, experts):
                if q == 1 or (isinstance(t, int) and t < 0):
                    pe.wait_ge(s.scores_done, B if isinstance(t, int) and t < PER else B - 1 + j)
                if experts:
                    m, e = experts
                    up(m, e)
                if on.load:
                    t_z(t, q, j)
                if experts and e:
                    down(m, e - 1)
                if on.hand:
                    wo(t)
                if on.fin:
                    t_g(t)
                if on.ffn:
                    lif2(t)
                if on.load:
                    rkv(t, on)
                if experts:
                    up(m, e + 1, (0,))
                if on.hand:
                    t_x1(t)
                if experts:
                    up(m, e + 1, (1,))
                if on.hand:
                    lif1(t, q, on)
                if experts:
                    down(m, e)

            def prepare(m, j):
                t = j * PER + PER
                pe.wait_ge(s.x3n_done, t - LAG_G + 1)
                pe.wait_ge(s.in_b, upto(t))
                pe.wait_ge(s.in_c, upto(t - 2))
                router_in(m)

            def finish(m, coming, mixed):
                if mixed:
                    down(m, E - 1)
                if coming is not None:
                    t = (coming - B + 1) * PER + PER
                    pe.wait_ge(s.in_a, upto(t + 2))
                    pe.wait_ge(s.g_copied, t - LAG_G + 1)
                    router(coming)

            def experts(m, e):
                up(m, e)
                if e:
                    down(m, e - 1)

            spiking_block(pe, Steps(pe, None), sub, prepare, experts, finish)

        @block.scalar
        def _(act):
            st = Steps(act, s.act_steps)
            activation = nc.scalar.activation

            def silus(m, e):
                for c in range(CHUNKS):
                    act.wait_ge(s.up_ready, m * 4 * E + 4 * e + 2 * c + 1)
                    if not (is_first(m) and e == 0):
                        act.wait_ge(s.gated, m * 2 * E + 2 * e + c - 1)
                    activation(silu[:, c], up_banks[c][0][:, 0:N], ACT.Silu).then_inc(s.silu_done, 1)

            def router_hi(m):
                act.wait_ge(s.xT_ps, m + 1)
                activation(x_hi[:], side2[:, 0:N], ACT.Copy).then_inc(s.hi_done, 1)

            def top_weights(m):
                act.wait_ge(s.lead_done, m + 1)
                activation(lead_tanh[:], lead[:], ACT.Tanh, scale=0.5).then_inc(s.tanh_done, 1)
                act.wait_ge(s.tanh_done, m + 1)
                for k in range(TOP):
                    last = activation(top_w[:, k], lead_tanh[:], ACT.Copy, scale=0.5 - k, bias=0.5)
                last.then_inc(s.top_done, 1)

            def copy_xT(b):
                act.wait_ge(s.xnT_ps, b + 1)
                activation(xnT[:], side0[:, 0:N], ACT.Copy).then_inc(s.xnT_done, 1)

            def copy_qkv(b, tiles):
                if not is_first(b):
                    act.wait_ge(s.qT_ps, b)
                for j in tiles:
                    act.wait_ge(s.qkv_ps, b * TILES + j + 1)
                    ps = (side1, side2)[j % 2]
                    activation(qk[:, j].rearrange("p h d -> p (h d)"), ps[:, 0:2 * C], ACT.Relu)
                    activation(v_one[:, j, 0:C], ps[:, 2 * C:3 * C], ACT.Copy).then_inc(s.qkv_out, 1)

            def copy_qT(b):
                act.wait_ge(s.qT_ps, b + 1)
                activation(qT[:], side1[:, 0:N], ACT.Copy).then_inc(s.qT_done, 1)

            def conv_centre(b):
                act.wait_ge(s.att_done, b + 1)
                activation(conv[:], att[:, 1:N + 1], ACT.Identity, scale=centre_w[:, 0:1],
                           bias=cols[:, DWB:DWB + 1]).then_inc(s.conv_mid, 1)

            act.wait_ge(s.load_c, 16 * LOADS_C)
            activation(half_b1[:], cols[:, B1:B1 + FCH], ACT.Copy, scale=HALF)
            activation(half_b2[:], cols[:, B2:B2 + 1], ACT.Copy, scale=HALF)
            st.did(activation(centre_w[:], cols[:, DW + 1:DW + 2], ACT.Copy, bias=1.0))
            st.settle()

            def slot(k, a, c):
                if k == 1 and a is not None:
                    copy_xT(a)
                if k == 2 and a is not None:
                    copy_qkv(a, (0, 1))
                if k == 3 and a is not None:
                    copy_qkv(a, (2, 3))

            def end(a, c, closing):
                if a is not None:
                    copy_qT(a)
                if c is not None:
                    router_hi(c)

            def expert(b, e, beside):
                if e == 2 and not (isinstance(b, int) and b + 1 >= B):
                    conv_centre(b + 1)
                silus(b, e)
                if e == 0:
                    top_weights(b)
                beside()

            def lead_in(k):
                if k == 1:
                    conv_centre(0)
                if k == 3:
                    act.wait_ge(s.load_w, 16 * LOADS_W)
                    for e in range(E):
                        activation(experts_hi[:, e], experts_f[:, e], ACT.Copy)
                    activation(gate_hi[:], gate_f[:], ACT.Copy).then_inc(s.hi_split, 1)

            def loop(start, last, batch):
                with act.Fori(start, last) as b:
                    batch(b)

            first_half(lead_in, slot, end, expert, lambda b: None, lambda b, e: None, loop)

            def fill(t, q, first, n, src, **how):
                if not (isinstance(t, int) and t < 1):
                    act.wait_ge(s.lif_steps, t * 2 * STEPS)
                dst = lif_in[:, (q + 1) % 2, first:first + n].rearrange("p a t -> p (a t)")
                return activation(dst, src, ACT.Identity, scale=HALF, **how)

            def sub(t, q, j, on, experts):
                if experts:
                    m, e = experts
                    silus(m, e)
                if on.fin:
                    act.wait_ge(s.g_ps, t - LAG_G + 1)
                if on.load:
                    act.wait_ge(s.zT_ps, t + 2)
                    activation(zT[:], side0[:, 0:P], ACT.Copy).then_inc(s.zT_done, 1)
                if on.fin:
                    activation(g_tok[:], side0[:, P:2 * P], ACT.Copy).then_inc(s.g_copied, 1)
                if on.ffn:
                    act.wait_ge(s.lif2_ps, t - 2)
                    fill(t, q, CC, B, side2[:, 0:P], bias=half_b2[:, 0:1]).then_inc(s.in_c, 1)
                if on.load:
                    act.wait_ge(s.rkv_ps, t + 2)
                    fill(t, q, CA, 3 * B, side0[:, 0:3 * P]).then_inc(s.in_a, 1)
                if on.hand:
                    act.wait_ge(s.x1T_ps, t)
                    activation(x1T_ring[:, (q - 1) % PER], side1[:, 0:P], ACT.Identity, scale=cols[:, LN1G:LN1G + 1],
                               bias=cols[:, LN1B:LN1B + 1]).then_inc(s.x1T_done, 1)
                if experts and not e:
                    top_weights(m)
                if experts:
                    silus(m, e + 1)
                if on.hand:
                    act.wait_ge(s.lif1_ps, t)
                    for k in range(FCH):
                        last = fill(t, q, CB + k * B, B, side2[:, k * P:(k + 1) * P], bias=half_b1[:, k:k + 1])
                    last.then_inc(s.in_b, 1)

            def experts(m, e):
                silus(m, e)
                if e == 0:
                    top_weights(m)

            spiking_block(act, Steps(act, None), sub, lambda m, j: router_hi(m), experts,
                          lambda m, coming, mixed: None)

        @block.gpsimd
        def _(pool):
            st = Steps(pool, s.pool_steps)
            g = nc.gpsimd
            g.memset(minus_half[:], -0.5)
            g.memset(v_one[:, :, C:C + 1], 1.0)
            g.memset(att[:, 0:1], 0.0)
            g.memset(att[:, N + 1:N + 2], 0.0)
            g.memset(lif_in[:], 0.0)
            g.memset(lif_v[:], 0.0)
            g.memset(h_decay[:], DECAY)
            st.did(g.memset(h_out[:], 0.0))
            st.settle()
            g.memset(h_decay[:, :, 0:1], 0.0).then_inc(s.zeros, 1)

            def rstd(ln, k):
                wait_apart(pool, ln.has_var, k + 1)
                st.did(g.tensor_scalar(ln.var[:], ln.mv[:, :, 1], LN_EPS, None, ALU.add))
                st.settle()
                n = ln.var.shape[1]
                g.tensor_tensor(ln.rstd[:], ln.var[:], minus_half[:, 0:n], ALU.pow).then_inc(ln.has_rstd, 1)

            def start_sum(m, phase1):
                if phase1:
                    pool.wait_ge(s.res_done, m + 1)
                else:
                    pool.wait_ge(s.x3_done, (m - B + 1) * PER)
                if not is_first(m):
                    wait_apart(pool, s.added, m * (E + 1))
                g.tensor_copy(acc[:], res[:]).then_inc(s.added, 1)

            def add(m, e, phase1):
                pool.wait_ge(s.y_weighted, m * E + e + 1)
                pool.wait_ge(s.added, m * (E + 1) + 1 + e)
                last = e == E - 1
                if last:
                    if phase1 and not is_first(m):
                        pool.wait_ge(s.x2_stored, 16 * m)
                        pool.wait_ge(s.z_done, m)
                    elif not phase1 and isinstance(m, int) and m == B:
                        pool.wait_ge(s.x2_stored, 16 * B)
                        pool.wait_ge(s.z_done, B)
                    elif not phase1:
                        pool.wait_ge(s.out_stored, (m - B) * 16 * PER)
                g.tensor_tensor((moe_out if last else acc)[:], acc[:], weighted[:, e % 2], ALU.add)\
                 .then_inc(s.added, 1)

            def add_bias(b):
                pool.wait_ge(s.x_loaded, 16 * (b + 1))
                if not is_first(b):
                    pool.wait_ge(s.res_done, b)
                for j in range(TILES):
                    last = g.tensor_tensor(x_plus_b[:, j], x_tok[:, j], proj_b[:], ALU.add)
                last.then_inc(s.xb_done, 1)

            def cube(b):
                pool.wait_ge(s.qk_first, b + 1)
                st.did(g.tensor_tensor(qk2[:], qk[:], qk[:], ALU.mult))
                st.settle()
                g.tensor_tensor(qk2[:], qk2[:], qk[:], ALU.mult).then_inc(s.cubed, 1)

            def slot(k, a, c):
                if k == 0 and a is not None:
                    rstd(ln_x, a)
                if k == 5:
                    if a is not None:
                        cube(a)
                    if c is not None:
                        rstd(ln_r, c)
                if k == 6 and a is not None:
                    add_bias(a)

            def expert(b, e, beside):
                if e == 0:
                    start_sum(b, True)
                else:
                    add(b, e - 1, True)
                beside()

            def rest(b, e):
                if e == 2 and not is_first(b):
                    rstd(ln_z, b - 1)

            pool.wait_ge(s.load_c, 16 * LOADS_C)
            first_half(lambda k: None, slot, lambda a, c, closing: closing(), expert,
                       lambda b: add(b, E - 1, True), rest,
                       lambda start, last, batch: rounds(pool, st, start, last, batch, 4))
            rstd(ln_z, B - 1)

            def sub(t, q, j, on, experts):
                if experts:
                    m, e = experts
                    if e == 0:
                        start_sum(m, False)
                if on.hand:
                    rstd(ln_a, t - 1)
                if on.fin:
                    c = t - LAG_G
                    place = (q - LAG_G) % PER
                    rstd(ln_g, c)
                    pool.wait_ge(s.g_normed, c + 1)
                    st.did(g.tensor_tensor(g_s[:], g_n[:], ln2_g[:], ALU.mult))
                    st.settle()
                    st.did(g.tensor_tensor(g_s[:], g_s[:], ln2_b[:], ALU.add))
                    st.settle()
                    pool.wait_ge(x2_loaded[place], 16 * j)
                    g.tensor_tensor(res[:, place], g_s[:], x2_ring[:, place], ALU.add).then_inc(s.x3_done, 1)
                if experts and e:
                    add(m, e - 1, False)
                if on.fin:
                    rstd(ln_m, c)
                if experts:
                    add(m, e, False)

            def sums(m, e):
                if e == 0:
                    start_sum(m, False)
                else:
                    add(m, e - 1, False)

            def finish(m, coming, mixed):
                if mixed:
                    add(m, E - 1, False)

            spiking_block(pool, st, sub, lambda m, j: None, sums, finish)

        @block.vector
        def _(dve):
            st = Steps(dve, s.dve_steps)
            v = nc.vector

            def gate_product(m, e, c):
                dve.wait_ge(s.silu_done, m * 2 * E + 2 * e + c + 1)
                dve.wait_ge(s.up_ready, m * 4 * E + 4 * e + 2 * c + 2)
                v.tensor_tensor(hidden[:, e % 2, c], silu[:, c], up_banks[c][1][:, 0:N], ALU.mult)\
                 .then_inc(s.gated, 1)

            def gate_products(m, e):
                for c in range(CHUNKS):
                    gate_product(m, e, c)

            def weigh(m, e):
                dve.wait_ge(s.down_ready, m * E + e + 1)
                if not (is_first(m) and e < 2):
                    dve.wait_ge(s.added, m * (E + 1) + (e - 1 if e < 2 else e))
                if e == 0:
                    dve.wait_ge(s.comb_done, m + 1)
                v.tensor_tensor(weighted[:, e % 2], down_bank[:, 0:N].rearrange("p (j c) -> p j c", c=C),
                                comb[:, :, e:e + 1].to_broadcast([P, TILES, C]), ALU.mult).then_inc(s.y_weighted, 1)

            def stats(ln, src, n):
                for j in range(n):
                    ins = v.bn_stats(ln.stats[:, j], src(j))
                st.did(ins)
                st.settle(wait_apart)
                for j in range(n):
                    ins = v.bn_aggr(ln.mv[:, j], ln.stats[:, j])
                ins.then_inc(ln.has_var, 1)

            def normalise(ln, k, dst, src, n, done):
                dve.wait_ge(ln.has_rstd, k + 1)
                for j in range(n):
                    ins = v.tensor_scalar(dst(j), src(j), ln.mv[:, j, 0:1], ln.rstd[:, j:j + 1],
                                          ALU.subtract, ALU.mult)
                ins.then_inc(done, 1)

            def router_lo(m):
                dve.wait_ge(s.hi_done, m + 1)
                v.tensor_tensor(x_lo[:], side2[:, 0:N], x_hi[:].bitcast(fp32), ALU.subtract).then_inc(s.lo_done, 1)

            def copy_scores(m):
                dve.wait_ge(s.router_ps, m + 1)
                v.tensor_copy(scores[:].rearrange("p j e -> p (j e)"), side0[:, 0:TILES * E])\
                 .then_inc(s.scores_done, 1)

            def route_steps(m):
                def find():
                    wait_apart(dve, s.scores_done, m + 1)
                    for j in range(TILES):
                        ins = v.max(best[:, j], scores[:, j])
                    st.did(ins)

                def compare():
                    st.settle()
                    v.tensor_tensor(lead[:], best[:, :, 0], best[:, :, 1], ALU.subtract).then_inc(s.lead_done, 1)
                    for j in range(TILES):
                        ins = v.max_index(best_no[:, j], best[:, j], scores[:, j])
                    st.did(ins)

                def number():
                    st.settle()
                    st.did(v.tensor_copy(best_nof[:], best_no[:, :, 0:TOP]))

                def match():
                    st.settle()
                    for k in range(TOP):
                        ins = v.tensor_tensor(pick[:, k], expert_no[:].unsqueeze(1).to_broadcast([P, TILES, E]),
                                              best_nof[:, :, k:k + 1].to_broadcast([P, TILES, E]), ALU.is_equal)
                    st.did(ins)

                def weight():
                    dve.wait_ge(s.top_done, m + 1)
                    st.settle()
                    for k in range(TOP):
                        ins = v.tensor_tensor(pick[:, k], pick[:, k],
                                              top_w[:, k].unsqueeze(2).to_broadcast([P, TILES, E]), ALU.mult)
                    st.did(ins)

                def combine():
                    st.settle()
                    v.tensor_tensor(comb[:], pick[:, 0], pick[:, 1], ALU.add).then_inc(s.comb_done, 1)

                return [find, compare, number, match, weight, combine]

            def route(m):
                for step in route_steps(m):
                    step()

            def norm_x(b):
                dve.wait_ge(s.x_loaded, 16 * (b + 1))
                stats(ln_x, lambda j: x_tok[:, j], TILES)

            def norm_x2(b):
                if not is_first(b):
                    dve.wait_ge(s.xnT_ps, b)
                normalise(ln_x, b, lambda j: xn[:, j], lambda j: x_tok[:, j], TILES, s.xn_done)

            def merge(t):
                return t[:].rearrange("p j h d -> p (j h) d")

            def inv():
                return qk_inv[:].rearrange("p j h -> p (j h)").unsqueeze(2).to_broadcast([P, TILES * 2 * HEADS, HD])

            def qk_sums(b):
                dve.wait_ge(s.qkv_out, (b + 1) * TILES)
                flat = qk[:].rearrange("p j h d -> p (j h d)")
                st.did(v.tensor_scalar(flat, flat, ATT_EPS, None, ALU.add))
                st.settle()
                st.did(v.tensor_reduce(qk_sum[:], qk[:], axis=AX, op=ALU.add))
                st.settle()
                st.did(v.reciprocal(qk_inv[:], qk_sum[:]))

            def qk_norm(b):
                st.settle()
                v.tensor_tensor(merge(qk), merge(qk), inv(), ALU.mult).then_inc(s.qk_first, 1)

            def cube_sums(b):
                dve.wait_ge(s.cubed, b + 1)
                st.did(v.tensor_reduce(qk_sum[:], qk2[:], axis=AX, op=ALU.add))
                st.settle()
                v.reciprocal(qk_inv[:], qk_sum[:]).then_inc(s.cubes_inverse, 1)

            def cube_norm(b):
                dve.wait_ge(s.cubes_inverse, b + 1)
                v.tensor_tensor(merge(qk), merge(qk2), inv(), ALU.mult).then_inc(s.qk_done, 1)

            def mask_kv(b):
                dve.wait_ge(s.kv_ps, b + 1)
                if not is_first(b):
                    dve.wait_ge(s.att_ps, b)
                v.tensor_tensor(kv_m[:], side0[:, 0:C], head_mask[:], ALU.mult)
                v.tensor_scalar(ks_m[:], head_mask[:], side0[:, C:C + 1], None, ALU.mult).then_inc(s.kv_masked, 1)

            def add_to_z(b):
                dve.wait_ge(s.att_ps, b + 1)
                v.tensor_scalar(z_inv[:], side0[:, 0:N], ATT_EPS, None, ALU.add).then_inc(s.z_added, 1)
                dve.wait_ge(s.z_added, b + 1)
                v.reciprocal(z_inv[:], z_inv[:]).then_inc(s.z_inverse, 1)

            def attended(b):
                dve.wait_ge(s.z_inverse, b + 1)
                v.tensor_tensor(att[:, 1:N + 1], side2[:, 0:N], z_inv[:], ALU.mult).then_inc(s.att_done, 1)

            def conv_sides(b):
                dve.wait_ge(s.conv_mid, b + 1)
                st.did(v.scalar_tensor_tensor(conv[:], att[:, 0:N], cols[:, DW:DW + 1], conv[:], ALU.mult, ALU.add))
                st.settle()
                v.scalar_tensor_tensor(conv[:], att[:, 2:N + 2], cols[:, DW + 2:DW + 3], conv[:], ALU.mult, ALU.add)\
                 .then_inc(s.conv_done, 1)

            def residual(b):
                dve.wait_ge(s.proj_ps, b + 1)
                dve.wait_ge(s.xb_done, b + 1)
                if not is_first(b):
                    dve.wait_ge(s.added, (b - 1) * (E + 1) + 1)
                v.tensor_tensor(res[:].rearrange("p j c -> p (j c)"), side1[:, 0:N],
                                x_plus_b[:].rearrange("p j c -> p (j c)"), ALU.add).then_inc(s.res_done, 1)
                dve.wait_ge(s.res_done, b + 1)
                stats(ln_r, lambda j: res[:, j], TILES)

            def norm_res(b):
                if not is_first(b):
                    dve.wait_ge(s.xT_ps, b)
                normalise(ln_r, b, lambda j: resn[:, j], lambda j: res[:, j], TILES, s.resn_done)

            def norm_out_stats(b):
                dve.wait_ge(s.added, b * (E + 1) + E + 1)
                stats(ln_z, lambda j: moe_out[:, j], TILES)

            def norm_out(b):
                if not is_first(b):
                    dve.wait_ge(s.z_stored, 16 * b)
                normalise(ln_z, b, lambda j: z_tok[:, j], lambda j: moe_out[:, j], TILES, s.z_done)

            def slot(k, a, c):
                if k == 0:
                    if a is not None:
                        norm_x(a)
                    if c is not None:
                        add_to_z(c)
                if k == 1:
                    if a is not None:
                        norm_x2(a)
                    if c is not None:
                        attended(c)
                if k == 2 and c is not None:
                    conv_sides(c)
                if k == 4 and a is not None:
                    qk_sums(a)
                if k == 5:
                    if a is not None:
                        qk_norm(a)
                    if c is not None:
                        residual(c)
                if k == 6 and a is not None:
                    cube_sums(a)
                if k == 7:
                    if c is not None:
                        norm_res(c)
                    if a is not None and c is None:
                        cube_norm(a)

            def end(a, c, closing):
                if a is not None:
                    if c is not None and is_first(c):
                        cube_norm(a)
                    mask_kv(a)
                if c is not None:
                    router_lo(c)
                closing()
                if c is not None:
                    copy_scores(c)

            def expert(b, e, beside):
                if e == E - 1 and not (isinstance(b, int) and b + 2 >= B):
                    cube_norm(b + 2)
                gate_products(b, e)
                if e == 0:
                    route(b)
                else:
                    weigh(b, e - 1)
                beside()

            def rest(b, e):
                if not is_first(b):
                    if e == 2:
                        norm_out_stats(b - 1)
                    if e == 3:
                        norm_out(b - 1)

            def lead_in(k):
                if k != 5:
                    return
                dve.wait_ge(s.hi_split, 1)
                v.tensor_tensor(experts_lo[:], experts_f[:], experts_hi[:].bitcast(fp32), ALU.subtract)
                v.tensor_tensor(gate_lo[:], gate_f[:], gate_hi[:].bitcast(fp32), ALU.subtract)\
                 .then_inc(s.lo_split, 1)
                st.did(v.tensor_copy(lif2_part[:, 0], lif2_f[:]))
                st.settle()
                st.did(v.tensor_tensor(lif2_rest[:], lif2_f[:], lif2_part[:, 0], ALU.subtract))
                st.settle()
                st.did(v.tensor_copy(lif2_part[:, 1], lif2_rest[:]))
                st.settle()
                st.did(v.tensor_tensor(lif2_rest[:], lif2_rest[:], lif2_part[:, 1], ALU.subtract))
                st.settle()
                v.tensor_copy(lif2_part[:, 2], lif2_rest[:]).then_inc(s.lo_split, 1)

            dve.wait_ge(s.zeros, 1)
            dve.wait_ge(s.load_c, 16 * LOADS_C)
            first_half(lead_in, slot, end, expert, lambda b: weigh(b, E - 1), rest,
                       lambda start, last, batch: rounds(dve, st, start, last, batch, 13))
            norm_out_stats(B - 1)
            norm_out(B - 1)

            def sub(t, q, j, on, experts):
                if not on.scan and not on.fin:
                    return
                now, old = lif_u[:, q % 2], lif_u[:, (q + 1) % 2]
                source = lif_in[:, q % 2]
                if experts:
                    m, e = experts

                def carry_in():
                    v.tensor_copy(kv_in[:, :, 0:1], h_out[:, :, STEPS:STEPS + 1])
                    st.did(v.tensor_scalar(v_spike[:], old[:, 2 * B:3 * B], V_TH, None, ALU.is_ge))

                def spikes_kv():
                    st.settle()
                    st.did(v.scalar_tensor_tensor(kv_in[:, :, 1:], old[:, B:2 * B], V_TH, v_spike[:],
                                                  ALU.is_ge, ALU.mult))

                def scan_h():
                    st.settle()
                    st.did(v.tensor_tensor_scan(h_out[:].rearrange("p b t -> p (b t)"),
                                                h_decay[:].rearrange("p b t -> p (b t)"),
                                                kv_in[:].rearrange("p b t -> p (b t)"), 0.0, ALU.mult, ALU.add))

                def gate_h():
                    st.settle()
                    if not (isinstance(t, int) and t < 2):
                        dve.wait_ge(s.wo_ps, t - 1)
                    v.scalar_tensor_tensor(y_fm[:].rearrange("p (b t) -> p b t", b=B), old[:, 0:B], V_TH,
                                           h_out[:, :, 1:], ALU.is_ge, ALU.mult).then_inc(s.y_done, 1)

                def ffn_spikes():
                    if not (isinstance(t, int) and t < 4):
                        dve.wait_ge(s.lif2_ps, t - 3)
                    v.tensor_scalar(s1[:].rearrange("p k t -> p (k t)"),
                                    old[:, CB:CB + FCH * B].rearrange("p a t -> p (a t)"), V_TH, None, ALU.is_ge)\
                     .then_inc(s.s1_done, 1)

                def final_sum():
                    if not (isinstance(t, int) and t < LAG_G + 1):
                        dve.wait_ge(s.g_ps, t - LAG_G)
                    v.scalar_tensor_tensor(gT[:], old[:, CC:CC + B].rearrange("p a t -> p (a t)"), V_TH,
                                           x1T_ring[:, (q - LAG_G) % PER], ALU.is_ge, ALU.add).then_inc(s.g_done, 1)

                def x1_sum():
                    dve.wait_ge(s.wo_ps, t)
                    v.tensor_tensor(x1p[:], side1[:, 0:C], z_ring[:, (q - 1) % PER], ALU.add).then_inc(s.x1p_done, 1)

                def x1_stats():
                    dve.wait_ge(s.x1p_done, t)
                    st.did(v.bn_stats(ln_a.stats[:, 0], x1p[:]))

                def x1_aggr():
                    st.settle(wait_apart)
                    v.bn_aggr(ln_a.mv[:, 0], ln_a.stats[:, 0]).then_inc(ln_a.has_var, 1)

                def x1_norm():
                    normalise(ln_a, t - 1, lambda j: x1n[:], lambda j: x1p[:], 1, s.x1n_done)

                def g_stats():
                    dve.wait_ge(s.g_copied, t - LAG_G + 1)
                    st.did(v.bn_stats(ln_g.stats[:, 0], g_tok[:]))

                def g_aggr():
                    st.settle(wait_apart)
                    v.bn_aggr(ln_g.mv[:, 0], ln_g.stats[:, 0]).then_inc(ln_g.has_var, 1)

                def g_norm():
                    normalise(ln_g, t - LAG_G, lambda j: g_n[:], lambda j: g_tok[:], 1, s.g_normed)

                def m_stats():
                    dve.wait_ge(s.x3_done, t - LAG_G + 1)
                    st.did(v.bn_stats(ln_m.stats[:, 0], res[:, (q - LAG_G) % PER]))

                def m_aggr():
                    st.settle(wait_apart)
                    v.bn_aggr(ln_m.mv[:, 0], ln_m.stats[:, 0]).then_inc(ln_m.has_var, 1)

                def m_norm():
                    place = (q - LAG_G) % PER
                    normalise(ln_m, t - LAG_G, lambda j: resn[:, place], lambda j: res[:, place], 1, s.x3n_done)

                fill = []

                def at(slot, *ops):
                    fill.append((slot, ops))

                if on.fin:
                    at(0, final_sum)
                if on.hand:
                    at(1, carry_in)
                    at(2, spikes_kv)
                    at(3, scan_h)
                    at(4, gate_h)
                if on.ffn:
                    at(5, ffn_spikes)
                if experts:
                    at(6, lambda: gate_product(m, e, 0))
                    at(7, lambda: gate_product(m, e, 1))
                if on.hand:
                    at(8, x1_sum)
                    at(9, x1_stats)
                    at(10, x1_aggr)
                if on.fin:
                    at(11, g_stats)
                    at(12, g_aggr)
                if experts and e:
                    at(13, lambda: weigh(m, e - 1))
                if on.hand:
                    at(14, x1_norm)
                if on.fin:
                    at(16, g_norm)
                if experts and not e:
                    for n, step in enumerate(route_steps(m)):
                        at(15 + 2 * n, step)
                if experts:
                    at(20, lambda: gate_product(m, e + 1, 0))
                    at(24, lambda: gate_product(m, e + 1, 1))
                if on.fin:
                    at(22, m_stats)
                    at(23, m_aggr)
                    at(27, m_norm)
                if experts:
                    at(29, lambda: weigh(m, e))

                def side(slot):
                    for when, ops in fill:
                        if when == slot:
                            for op in ops:
                                op()

                if on.load or on.hand:
                    dve.wait_ge(s.in_a, upto(t + 1))
                if not (isinstance(t, int) and t < 2):
                    dve.wait_ge(s.in_b, upto(t - 1))
                if not (isinstance(t, int) and t < 4):
                    dve.wait_ge(s.in_c, upto(t - 3))
                for i in range(STEPS):
                    if on.scan:
                        if not (i == 0 and is_first(t)):
                            dve.wait_ge(s.lif_steps, t * 2 * STEPS + 2 * i)
                        v.scalar_tensor_tensor(now[:, :, i], lif_v[:], HALF, source[:, :, i], ALU.mult, ALU.add)\
                         .then_inc(s.lif_steps, 1)
                    side(2 * i)
                    if on.scan:
                        dve.wait_ge(s.lif_steps, t * 2 * STEPS + 2 * i + 1)
                        v.scalar_tensor_tensor(lif_v[:], now[:, :, i], V_TH, now[:, :, i], ALU.is_lt, ALU.mult)\
                         .then_inc(s.lif_steps, 1)
                    side(2 * i + 1)

            def experts_alone(m, e):
                gate_products(m, e)
                if e:
                    weigh(m, e - 1)
                else:
                    route(m)

            def finish(m, coming, mixed):
                if mixed:
                    weigh(m, E - 1)
                if coming is not None:
                    copy_scores(coming)

            spiking_block(dve, st, sub, lambda m, j: router_lo(m), experts_alone, finish)

    return nc


def kernel(**inputs):
    import numpy as np
    import concourse.bacc as bacc
    from concourse.bass_utils import run_bass_kernel_spmd

    a, b, f = "L0_attn_a_", "L0_attn_b_", "L0_ffn_"
    given = {k: np.asarray(v) for k, v in inputs.items()}
    p = np.arange(128)

    def columns(v):
        return v.reshape(-1, 128).T

    arrays = {
        "x": given[a + "x"],
        "qkv_w": given[a + "w_qkv"].T,
        "proj_w": given[a + "w_proj"].T,
        "b_proj": given[a + "b_proj"],
        "wr": given[b + "Wr"].T,
        "wk": given[b + "Wk"].T,
        "wv": given[b + "Wv"].T,
        "wo": given[b + "Wo"].T,
        "lif_w1": given[b + "W1"].T,
        "lif_w2": given[b + "W2"].T,
        "ln2_g": given[b + "ln2_g"],
        "ln2_b": given[b + "ln2_b"],
        "Wg": given[f + "Wg"],
        "W1": given[f + "W1"],
        "W3": given[f + "W3"],
        "W2": given[f + "W2"],
        "cols": np.concatenate([columns(given[b + "b1"]), columns(given[b + "b2"]), columns(given[b + "ln1_g"]),
                                columns(given[b + "ln1_b"]), given[a + "w_dwc"], columns(given[a + "b_dwc"])],
                               axis=1),
        "ident": np.eye(128, dtype=np.float32),
        "head_mask": (p[:, None] // 8 == p[None, :] // 8).astype(np.float32),
        "expert_no": np.tile(np.arange(8, dtype=np.float32), (128, 1)),
    }
    arrays = {k: np.ascontiguousarray(v) for k, v in arrays.items()}
    nc = bacc.Bacc("TRN2", target_bir_lowering=False, num_devices=1)
    dram, feeds = {}, {}
    for name, value in arrays.items():
        dram[name] = nc.dram_tensor(f"in_{name}", value.shape, mybir.dt.from_np(value.dtype),
                                    kind="ExternalInput").ap()
        feeds[f"in_{name}"] = value
    dram["out"] = nc.dram_tensor("out_x", arrays["x"].shape, mybir.dt.float32, kind="ExternalOutput").ap()
    build_program(nc, dram)
    done = run_bass_kernel_spmd(nc, [feeds], core_ids=[0])
    return done.results[0]["out_x"]
```

```python
import concourse.bass as bass
from concourse import mybir
from contextlib import ExitStack
from collections import namedtuple


LayerNorm = namedtuple("LayerNorm", "stats mv var rstd has_var has_rstd")
Stages = namedtuple("Stages", "load hand ffn fin scan")
Unit = namedtuple("Unit", "no routed tiles place")


class Steps:

    def __init__(self, eng, sem):
        self.eng, self.sem, self.n, self.base = eng, sem, 0, 0

    def did(self, instruction):
        instruction.then_inc(self.sem, 1)
        self.n += 1

    def settle(self, wait=None):
        if wait:
            wait(self.eng, self.sem, self.base + self.n)
        else:
            self.eng.wait_ge(self.sem, self.base + self.n)


def rounds(eng, steps, start, end, body, each=0):
    before = steps.n
    with eng.Fori(start, end) as i:
        steps.base = (i - start) * each
        body(i)
    assert steps.n == before + each, steps.n - before
    steps.n, steps.base = before + (end - start) * each, 0


def peeled(eng, steps, start, end, body):
    before = steps.n
    body(start)
    rounds(eng, steps, start + 1, end, body, steps.n - before)


def is_first(i):
    return isinstance(i, int) and i == 0


def build_program(nc, dram):
    fp32 = mybir.dt.float32
    fp32r = mybir.dt.float32r
    bf16 = mybir.dt.bfloat16
    u32 = mybir.dt.uint32
    ALU = mybir.AluOpType
    ACT = mybir.ActivationFunctionType
    AX = mybir.AxisListType.X

    x_in_dram, out_dram = dram["x"], dram["out"]
    B, N, C = x_in_dram.shape
    P = 128
    TILES = N // P
    E, _, HID = dram["W1"].shape
    CHUNKS = HID // P
    F = dram["lif_w1"].shape[1]
    FCH = F // P
    HEADS, HD = 16, 8
    TOP = 2
    LN_EPS, ATT_EPS = 1e-5, 1e-6
    V_TH, DECAY, HALF = 1.0, 0.9, 0.5
    STEPS = P // B
    SUBS = N // STEPS
    PER = 4
    COLS = (3 + FCH + 1) * B
    SCORES = slice(3 * P, 3 * P + TILES * E)
    CA, CB, CC = 0, 3 * B, (3 + FCH) * B
    LAG_C, LAG_G = 4, 5
    SPLIT = 3

    ctx = ExitStack()
    with ctx:
        def sb(name, shape, dt=fp32):
            return ctx.enter_context(nc.sbuf_tensor(name, shape, dt))

        def sem(name):
            return ctx.enter_context(nc.semaphore(name))

        experts_f = sb("experts_f", [P, E, 2 * HID])
        experts_hi = sb("experts_hi", [P, E, 2 * HID], fp32r)
        experts_lo = sb("experts_lo", [P, E, 2 * HID], fp32r)
        down_w = sb("down_w", [P, E, CHUNKS, C])
        gate_f = sb("gate_f", [P, E])
        gate_hi = sb("gate_hi", [P, E], fp32r)
        gate_lo = sb("gate_lo", [P, E], fp32r)
        qkv_w = sb("qkv_w", [P, 3 * C])
        proj_w = sb("proj_w", [P, C])
        rkv_w = sb("rkv_w", [P, 3, C])
        wo_w = sb("wo_w", [P, C])
        lif1_w = sb("lif1_w", [P, F])
        lif2_f = sb("lif2_f", [P, FCH, C])
        lif2_rest = sb("lif2_rest", [P, FCH, C])
        lif2_part = sb("lif2_part", [P, 3, FCH, C], bf16)
        ident = sb("ident", [P, P])
        head_mask = sb("head_mask", [P, P])
        expert_no = sb("expert_no", [P, E])
        cols = sb("cols", [P, FCH + 7])
        half_b1 = sb("half_b1", [P, FCH])
        half_b2 = sb("half_b2", [P, 1])
        centre_w = sb("centre_w", [P, 1])
        proj_b = sb("proj_b", [P, C])
        ln2_g = sb("ln2_g", [P, C])
        ln2_b = sb("ln2_b", [P, C])
        minus_half = sb("minus_half", [P, TILES])
        B1, B2, LN1G, LN1B, DW, DWB = 0, FCH, FCH + 1, FCH + 2, FCH + 3, FCH + 6

        res = sb("res", [P, TILES, C])
        resn = sb("resn", [P, TILES, C])
        x_hi = sb("x_hi", [P, SPLIT, N], fp32r)
        x_lo = sb("x_lo", [P, SPLIT, N], fp32r)
        silu = sb("silu", [P, CHUNKS, N])
        hidden = sb("hidden", [P, 2, CHUNKS, N])
        weighted = sb("weighted", [P, 2, TILES, C])
        first = sb("first", [P, SPLIT, TILES, C])
        acc = sb("acc", [P, TILES, C])
        moe_out = sb("moe_out", [P, TILES, C])
        scores = sb("scores", [P, TILES, E])
        best = sb("best", [P, TILES, 8])
        best_no = sb("best_no", [P, TILES, 8], u32)
        best_nof = sb("best_nof", [P, TILES, TOP])
        lead = sb("lead", [P, TILES])
        lead_tanh = sb("lead_tanh", [P, TILES])
        top_w = sb("top_w", [P, TOP, TILES])
        pick = sb("pick", [P, TOP, TILES, E])
        comb = sb("comb", [P, SPLIT, TILES, E])

        def ln_set(name, n):
            return LayerNorm(stats=sb(name + "_stats", [P, n, 6]), mv=sb(name + "_mv", [P, n, 2]),
                             var=sb(name + "_var", [P, n]), rstd=sb(name + "_rstd", [P, n]),
                             has_var=sem(name + "_has_var"), has_rstd=sem(name + "_has_rstd"))

        ln_x = ln_set("ln_x", TILES)
        ln_r = ln_set("ln_r", TILES)
        ln_z = ln_set("ln_z", TILES)
        ln_a = ln_set("ln_a", 1)
        ln_g = ln_set("ln_g", 1)
        ln_m = ln_set("ln_m", 1)

        x_tok = sb("x_tok", [P, TILES, C])
        x_plus_b = sb("x_plus_b", [P, TILES, C])
        xn = sb("xn", [P, TILES, C])
        xnT = sb("xnT", [P, N])
        qk = sb("qk", [P, TILES, 2 * HEADS, HD])
        qk2 = sb("qk2", [P, TILES, 2 * HEADS, HD])
        qk_sum = sb("qk_sum", [P, TILES, 2 * HEADS])
        qk_inv = sb("qk_inv", [P, TILES, 2 * HEADS])
        v_one = sb("v_one", [P, TILES, C + 1])
        kv_m = sb("kv_m", [P, C])
        ks_m = sb("ks_m", [P, C])
        qT = sb("qT", [P, N])
        z_inv = sb("z_inv", [P, N])
        att = sb("att", [P, N + 2])
        conv = sb("conv", [P, N])
        z_tok = sb("z_tok", [P, TILES, C])

        lif_in = sb("lif_in", [P, 2, COLS, STEPS])
        lif_u = sb("lif_u", [P, 2, COLS, STEPS])
        lif_v = sb("lif_v", [P, COLS])
        z_ring = sb("z_ring", [P, PER, C])
        x2_ring = sb("x2_ring", [P, PER, C])
        x1T_ring = sb("x1T_ring", [P, PER, P])
        zT = sb("zT", [P, P])
        v_spike = sb("v_spike", [P, B, STEPS])
        kv_in = sb("kv_in", [P, B, STEPS + 1])
        h_out = sb("h_out", [P, B, STEPS + 1])
        h_decay = sb("h_decay", [P, B, STEPS + 1])
        y_fm = sb("y_fm", [P, P])
        x1p = sb("x1p", [P, C])
        x1n = sb("x1n", [P, C])
        s1 = sb("s1", [P, FCH, P], bf16)
        gT = sb("gT", [P, P])
        g_tok = sb("g_tok", [P, C])
        g_n = sb("g_n", [P, C])
        g_s = sb("g_s", [P, C])

        def bank(name):
            return ctx.enter_context(nc.psum_tensor(name, [P, 512], fp32))

        up_banks = [[bank("up_a1"), bank("up_a3")], [bank("up_b1"), bank("up_b3")]]
        down_bank = bank("down_bank")
        side0, side1, side2 = bank("side0"), bank("side1"), bank("side2")

        signals = """
            load_w load_c x_loaded zeros hi_split lo_split
            up_ready silu_done gated down_ready y_weighted sum_started added
            xT_ps hi_done lo_done router_ps scores_done lead_done tanh_done top_done comb_done
            xn_done xnT_ps xnT_done qkv_ps qkv_out qk_first cubed cubes_inverse qk_done kv_ps kv_masked qT_ps qT_done
            att_ps z_added z_inverse att_done conv_mid conv_done proj_ps xb_done res_done resn_done
            z_done x2_stored z_stored
            zT_ps zT_done rkv_ps in_a y_done wo_ps x1p_done x1n_done x1T_ps x1T_done lif1_ps in_b
            s1_done lif2_ps in_c g_done g_ps g_copied g_normed x3_done x3n_done
            lif_steps dve_steps act_steps pool_steps out_stored""".split()
        s = namedtuple("Signals", signals)(*[sem(n) for n in signals])

        z_loaded = [sem(f"z_loaded{q}") for q in range(PER)]
        x2_loaded = [sem(f"x2_loaded{q}") for q in range(PER)]

        x2_dram = nc.dram_tensor("x2_scratch", (B, N, C), fp32, kind="Internal").ap()
        z_dram = nc.dram_tensor("z_scratch", (B, N, C), fp32, kind="Internal").ap()

        def rows_of_batch(t, b):
            return t[bass.ds(b, 1)].rearrange("o (j p) c -> p (o j) c", p=P)

        block = ctx.enter_context(nc.Block())
        LOADS_W, LOADS_C = 11, 8
        GROUPS = SUBS // PER

        def wait_apart(eng, which, count):
            if not isinstance(count, int):
                count = eng.to_reg(count)
                eng.wait_ge(s.zeros, 1)
            eng.wait_ge(which, count)

        ALL = range(TILES)
        HALVES = ALL[:TILES // 2], ALL[TILES // 2:]
        EARLY = [Unit(B - SPLIT + k, B - SPLIT + k, HALVES[0], k) for k in range(SPLIT)]
        LATE = [Unit(B + k, B - SPLIT + k, HALVES[1], k) for k in range(SPLIT)]
        UNITS = B + len(LATE)
        LATE_ENDS = [PER * k + 2 for k in range(len(LATE))]

        def unit_of_batch(b):
            return EARLY[b - B + SPLIT] if isinstance(b, int) and b >= B - SPLIT else Unit(b, b, ALL, 0)

        def unit_of_group(k):
            return Unit(UNITS + k, B + k, ALL, 0)

        def is_late(u):
            return any(u is late for late in LATE)

        def place_of(m):
            return m - B + SPLIT if isinstance(m, int) and B - SPLIT <= m < B else 0

        def span(u):
            return slice(u.tiles[0] * P, (u.tiles[-1] + 1) * P)

        def part(t, u):
            return t[:, u.tiles[0]:u.tiles[-1] + 1]

        def first_half(lead_in, slot, end, expert, closing, rest, loop):
            for a, c in ((0, None), (1, 0)):
                for k in range(E):
                    slot(k, a, c)
                    if c == 0:
                        lead_in(k)
                end(a, c, lambda: None)

            def batch(b):
                known = isinstance(b, int)
                a = None if known and b + 2 >= B else b + 2
                c = None if known and b + 1 >= B else b + 1
                u = unit_of_batch(b)
                for e in range(E):
                    expert(u, e, lambda: slot(e, a, c))
                    rest(b, e)
                end(a, c, lambda: closing(u))

            batch(0)
            loop(1, B - SPLIT, batch)
            for b in range(B - SPLIT, B):
                batch(b)

        def in_lead(a, c):
            return a is not None and (c is None or is_first(c))

        def stages(t):
            if not isinstance(t, int):
                return Stages(load=True, hand=True, ffn=True, fin=True, scan=True)
            return Stages(load=t + 1 < SUBS, hand=0 <= t - 1 < SUBS, ffn=0 <= t - 3 < SUBS,
                           fin=0 <= t - LAG_G < SUBS, scan=0 <= t < SUBS + LAG_C)

        def upto(n):
            return min(n, SUBS) if isinstance(n, int) else n

        def expert_before(u, e):
            if e:
                return u, e - 1
            if isinstance(u.no, int) and u.no <= UNITS:
                return (LATE[u.no - B - 1], E - 1) if u.no > B else None
            return Unit(u.no - 1, u.routed - 1, ALL, 0), E - 1

        def spiking_block(sub, loop, experts, finish):
            for e in range(E - 4):
                experts(LATE[0], e)
            sub(-1, PER - 1, -1, stages(-1), None, None)
            for e in range(E - 4, E - 2):
                experts(LATE[0], e)
            sub(0, 0, -1, stages(0), (LATE[0], E - 2), None)

            def unit(j):
                return LATE[j + 1] if isinstance(j, int) and j < 2 else unit_of_group(j - 2)

            def group(j):
                known = isinstance(j, int)
                u = unit(j)
                for i in range(PER):
                    t = j * PER + 1 + i
                    coming = None if i < PER - 1 or (known and j == 0) else B - 1 + j
                    sub(t, (1 + i) % PER, j, stages(t), (u, 2 * i), coming)

            for j in range(3):
                group(j)
            full = (SUBS - 2) // PER
            loop(3, full, group)
            for j in range(full, GROUPS + 1):
                group(j)
            last = unit(GROUPS + 1)
            for e in range(E):
                experts(last, e)
            finish(last)

        @block.sync
        def _(sp):
            for dst, src in ((ident[:], dram["ident"]), (head_mask[:], dram["head_mask"]),
                             (expert_no[:], dram["expert_no"]), (cols[:], dram["cols"]),
                             (proj_b[:], dram["b_proj"].partition_broadcast(P)),
                             (ln2_g[:], dram["ln2_g"].partition_broadcast(P)),
                             (ln2_b[:], dram["ln2_b"].partition_broadcast(P)),
                             (qkv_w[:], dram["qkv_w"])):
                sp.dma_start(dst, src).then_inc(s.load_c, 16)

            def load_x(b):
                if not is_first(b):
                    sp.wait_ge(s.xn_done, b)
                    sp.wait_ge(s.xb_done, b)
                sp.dma_start(x_tok[:], rows_of_batch(x_in_dram, b)).then_inc(s.x_loaded, 16)

            load_x(0)
            for dst, src in ((experts_f[:, :, 0:HID], dram["W1"].rearrange("e d h -> d e h")),
                             (experts_f[:, :, HID:], dram["W3"].rearrange("e d h -> d e h")),
                             (down_w[:], dram["W2"].rearrange("e (k p) d -> p e k d", p=P)),
                             (gate_f[:], dram["Wg"]), (proj_w[:], dram["proj_w"]),
                             (rkv_w[:, 0], dram["wr"]), (rkv_w[:, 1], dram["wk"]), (rkv_w[:, 2], dram["wv"]),
                             (wo_w[:], dram["wo"]), (lif1_w[:], dram["lif_w1"]),
                             (lif2_f[:], dram["lif_w2"].rearrange("(k p) d -> p k d", p=P))):
                sp.dma_start(dst, src).then_inc(s.load_w, 16)

            def rows_of_unit(t, u):
                return rows_of_batch(t, u.routed)[:, u.tiles[0]:u.tiles[-1] + 1]

            def store_x2(u):
                sp.wait_ge(s.added, (u.no + 1) * E)
                sp.dma_start(rows_of_unit(x2_dram, u), part(moe_out, u)).then_inc(s.x2_stored, 16)

            def store_z(u):
                sp.wait_ge(s.z_done, u.no + 1)
                sp.dma_start(rows_of_unit(z_dram, u), part(z_tok, u)).then_inc(s.z_stored, 16)

            load_x(1)
            load_x(2)

            def batch(b):
                store_x2(unit_of_batch(b))
                store_z(unit_of_batch(b))
                load_x(b + 4)

            load_x(3)
            batch(0)
            with sp.Fori(1, B - 4) as b:
                batch(b)
            for b in range(B - 4, B):
                store_x2(unit_of_batch(b))
                store_z(unit_of_batch(b))

            sp.wait_ge(s.x2_stored, 16 * B)
            sp.wait_ge(s.z_stored, 16 * B)

            def by_time(t, c):
                return t[:, bass.ds(c * STEPS, STEPS), :]

            def load_z(c, slot):
                if not isinstance(c, int) or c >= PER:
                    sp.wait_ge(s.x1p_done, c - PER + 1)
                sp.dma_start(z_ring[:, slot], by_time(z_dram, c)).then_inc(z_loaded[slot], 16)

            def load_x2(c, slot):
                if not isinstance(c, int) or c >= PER:
                    sp.wait_ge(s.x3_done, c - PER + 1)
                sp.dma_start(x2_ring[:, slot], by_time(x2_dram, c)).then_inc(x2_loaded[slot], 16)

            def store_out(k):
                sp.wait_ge(s.added, (UNITS + k + 1) * E)
                for q in range(PER):
                    sp.dma_start(by_time(out_dram, k * PER + q), moe_out[:, q]).then_inc(s.out_stored, 16)

            for c in range(PER):
                load_z(c, c)
            for c in range(PER):
                load_x2(c, c)

            def group(j):
                if not (isinstance(j, int) and j < 4):
                    store_out(j - 4)
                for q in range(PER):
                    load_z(j * PER + q, q)
                    if not (isinstance(j, int) and j < 2):
                        load_x2((j - 1) * PER + q, q)
                    if isinstance(j, int) and j <= len(LATE) and q == 1:
                        store_x2(LATE[j - 1])
                        store_z(LATE[j - 1])

            for j in range(1, 4):
                group(j)
            sp.wait_ge(s.x2_stored, 16 * UNITS)
            sp.wait_ge(s.z_stored, 16 * UNITS)
            with sp.Fori(4, GROUPS) as j:
                group(j)
            store_out(GROUPS - 4)
            for q in range(PER):
                load_x2((GROUPS - 1) * PER + q, q)
            for k in range(GROUPS - 3, GROUPS):
                store_out(k)
            sp.wait_ge(s.out_stored, 16 * SUBS)

        @block.tensor
        def _(pe):
            mm = nc.tensor.matmul

            def three(out, w_hi, w_lo, m_hi, m_lo):
                mm(out, w_lo, m_hi, start=True, stop=False)
                mm(out, w_hi, m_lo, start=False, stop=False)
                return mm(out, w_hi, m_hi, start=False, stop=True)

            def up(u, e, chunks=range(CHUNKS)):
                if e == 0:
                    pe.wait_ge(s.lo_done, u.routed + 1)
                for c in chunks:
                    if not (is_first(u.no) and e == 0):
                        pe.wait_ge(s.gated, u.no * 2 * E + 2 * e + c - 1)
                    for k in range(2):
                        lo = k * HID + c * P
                        three(up_banks[c][k][:, span(u)], experts_hi[:, e, lo:lo + P], experts_lo[:, e, lo:lo + P],
                              x_hi[:, u.place, span(u)], x_lo[:, u.place, span(u)]).then_inc(s.up_ready, 1)

            def split(tiles):
                half = len(tiles) // 2
                return tiles[:half], tiles[half:]

            def down(u, e, half=None):
                tiles = u.tiles if half is None else split(u.tiles)[half]
                if not half:
                    pe.wait_ge(s.gated, u.no * 2 * E + 2 * e + 2)
                    if not (is_first(u.no) and e == 0):
                        pe.wait_ge(s.y_weighted, u.no * E + e)
                for j in tiles:
                    for c in range(CHUNKS):
                        last = mm(down_bank[:, j * C:(j + 1) * C], hidden[:, e % 2, c, j * P:(j + 1) * P],
                                  down_w[:, e, c], start=(c == 0), stop=(c == CHUNKS - 1))
                if half != 0:
                    last.then_inc(s.down_ready, 1)

            def router_in(m, bank):
                for j in range(TILES):
                    last = nc.tensor.transpose(bank[:, j * P:(j + 1) * P], resn[:, j], ident[:])
                last.then_inc(s.xT_ps, 1)

            def router(m):
                pe.wait_ge(s.lo_done, m + 1)
                for j in range(TILES):
                    t = slice(j * P, (j + 1) * P)
                    at = SCORES.start + j * E
                    last = three(side0[:, at:at + E], x_hi[:, place_of(m), t], x_lo[:, place_of(m), t], gate_hi[:], gate_lo[:])
                last.then_inc(s.router_ps, 1)

            def t_x(b):
                pe.wait_ge(s.xn_done, b + 1)
                if not is_first(b):
                    pe.wait_ge(s.z_added, b)
                for j in range(TILES):
                    last = nc.tensor.transpose(side0[:, j * P:(j + 1) * P], xn[:, j], ident[:])
                last.then_inc(s.xnT_ps, 1)

            def qkv(b, tiles):
                pe.wait_ge(s.xnT_done, b + 1)
                for j in tiles:
                    if j >= 2:
                        pe.wait_ge(s.qkv_out, b * TILES + j - 1)
                    elif j == 1 and not is_first(b):
                        pe.wait_ge(s.att_done, b)
                    mm((side1, side2)[j % 2][:, 0:3 * C], xnT[:, j * P:(j + 1) * P], qkv_w[:],
                       start=True, stop=True).then_inc(s.qkv_ps, 1)

            def kv(b):
                pe.wait_ge(s.qk_done, b + 1)
                for j in range(TILES):
                    k_tile = qk[:, j, HEADS:2 * HEADS].rearrange("p h d -> p (h d)")
                    last = mm(side0[:, 0:C + 1], k_tile, v_one[:, j], start=(j == 0), stop=(j == TILES - 1))
                last.then_inc(s.kv_ps, 1)
                if not is_first(b):
                    pe.wait_ge(s.res_done, b)
                for j in range(TILES):
                    q_tile = qk[:, j, 0:HEADS].rearrange("p h d -> p (h d)")
                    last = nc.tensor.transpose(side1[:, j * P:(j + 1) * P], q_tile, ident[:])
                last.then_inc(s.qT_ps, 1)

            def attend(b):
                pe.wait_ge(s.kv_masked, b + 1)
                pe.wait_ge(s.qT_done, b + 1)
                if not is_first(b):
                    pe.wait_ge(s.scores_done, b)
                mm(side0[:, 0:N], ks_m[:], qT[:], start=True, stop=True)
                mm(side2[:, 0:N], kv_m[:], qT[:], start=True, stop=True).then_inc(s.att_ps, 1)

            def project(b, following):
                pe.wait_ge(s.conv_done, b + 1)
                if following is not None:
                    pe.wait_ge(s.qkv_out, (following + 1) * TILES)
                for j in range(TILES):
                    last = mm(side1[:, j * C:(j + 1) * C], conv[:, j * P:(j + 1) * P], proj_w[:],
                              start=True, stop=True)
                last.then_inc(s.proj_ps, 1)

            def slot(k, a, c):
                if k == 0 and c is not None:
                    attend(c)
                if k == 1 and a is not None:
                    t_x(a)
                if k == 2 and a is not None:
                    qkv(a, (0, 1))
                if k == 3 and a is not None:
                    qkv(a, (2, 3))
                if k == 4 and c is not None:
                    project(c, a)

            def end(a, c, closing):
                if in_lead(a, c) and c is not None:
                    pe.wait_ge(s.resn_done, c + 1)
                    pe.wait_ge(s.qkv_out, (a + 1) * TILES)
                    router_in(c, side2)
                    router(c)
                    pe.wait_ge(s.scores_done, c + 1)
                    kv(a)
                    return
                if a is not None:
                    kv(a)
                if c is not None:
                    pe.wait_ge(s.resn_done, c + 1)
                    router_in(c, side2)
                closing()
                if c is not None:
                    if a is not None:
                        pe.wait_ge(s.kv_masked, a + 1)
                    router(c)

            def expert(u, e, beside):
                up(u, e)
                if e:
                    down(u, e - 1)
                beside()

            def lead_in(k):
                if k == 3:
                    pe.wait_ge(s.load_w, 16 * LOADS_W)
                if k == E - 1:
                    pe.wait_ge(s.lo_split, 2)

            def loop(start, last, batch):
                with pe.Fori(start, last) as b:
                    batch(b)

            pe.wait_ge(s.load_c, 16 * LOADS_C)
            first_half(lead_in, slot, end, expert, lambda u: down(u, E - 1), lambda b, e: None, loop)

            def t_z(t, q, j):
                place = (q + 1) % PER
                pe.wait_ge(z_loaded[place], 16 * (j + (2 if place in (0, 1) else 1)))
                if not (isinstance(t, int) and t < 0):
                    pe.wait_ge(s.in_a, t + 1)
                nc.tensor.transpose(side0[:, 0:P], z_ring[:, place], ident[:]).then_inc(s.zT_ps, 1)

            def t_g(t):
                pe.wait_ge(s.g_done, t - LAG_G + 1)
                if not (isinstance(t, int) and t < LAG_G + 1):
                    pe.wait_ge(s.g_copied, t - LAG_G)
                nc.tensor.transpose(side0[:, P:2 * P], gT[:], ident[:]).then_inc(s.g_ps, 1)

            def rkv(t, on, r):
                pe.wait_ge(s.zT_done, t + 2)
                if on.fin:
                    pe.wait_ge(s.g_copied, t - LAG_G + 1)
                if r is not None:
                    pe.wait_ge(s.scores_done, r + 1)
                for k in range(3):
                    last = mm(side0[:, k * P:(k + 1) * P], rkv_w[:, k], zT[:], start=True, stop=True)
                last.then_inc(s.rkv_ps, 1)

            def wo(t):
                pe.wait_ge(s.y_done, t)
                if not (isinstance(t, int) and t < 2):
                    pe.wait_ge(s.x1T_done, t - 1)
                mm(side1[:, 0:C], y_fm[:], wo_w[:], start=True, stop=True).then_inc(s.wo_ps, 1)

            def t_x1(t):
                pe.wait_ge(s.x1n_done, t)
                nc.tensor.transpose(side1[:, 0:P], x1n[:], ident[:]).then_inc(s.x1T_ps, 1)

            def lif1(t, q, on):
                pe.wait_ge(s.x1T_done, t)
                if on.ffn:
                    pe.wait_ge(s.in_c, t - 2)
                elif t > 1:
                    pe.wait_ge(s.in_b, t - 1)
                for k in range(FCH):
                    last = mm(side2[:, k * P:(k + 1) * P], lif1_w[:, k * P:(k + 1) * P], x1T_ring[:, (q - 1) % PER],
                              start=True, stop=True)
                last.then_inc(s.lif1_ps, 1)

            def lif2(t):
                if isinstance(t, int) and t == 3:
                    pe.wait_ge(s.lo_split, 3)
                pe.wait_ge(s.s1_done, t - 2)
                pe.wait_ge(s.in_b, upto(t - 1))
                if not (isinstance(t, int) and t < 4):
                    pe.wait_ge(s.in_c, t - 3)
                for k in range(FCH):
                    for part in range(3):
                        last = mm(side2[:, 0:P], lif2_part[:, 2 - part, k], s1[:, k],
                                  start=(k == 0 and part == 0), stop=(k == FCH - 1 and part == 2))
                last.then_inc(s.lif2_ps, 1)

            def sub(t, q, j, on, experts, coming):
                if isinstance(t, int) and t < 0:
                    pe.wait_ge(s.scores_done, B)
                u, e = experts or (None, None)
                r = u.routed if e == 0 and not is_late(u) else None
                if experts:
                    up(u, e)
                if on.load:
                    t_z(t, q, j)
                if on.fin:
                    t_g(t)
                if experts and expert_before(u, e):
                    down(*expert_before(u, e))
                if on.hand:
                    wo(t)
                if r is not None:
                    if on.load:
                        pe.wait_ge(s.zT_done, t + 2)
                    if on.fin:
                        pe.wait_ge(s.g_copied, t - LAG_G + 1)
                    router(r)
                    up(u, e + 1, range(1))
                if on.load:
                    rkv(t, on, r)
                if r is not None:
                    up(u, e + 1, range(1, CHUNKS))
                elif experts:
                    up(u, e + 1)
                if on.ffn:
                    lif2(t)
                if on.hand:
                    t_x1(t)
                if experts:
                    down(u, e, 0)
                if coming is not None:
                    pe.wait_ge(s.x3n_done, (coming - B + 1) * PER)
                    pe.wait_ge(s.x1T_done, upto(t))
                    router_in(coming, side1)
                if on.hand:
                    lif1(t, q, on)
                if experts:
                    down(u, e, 1)

            def experts(u, e):
                up(u, e)
                if expert_before(u, e):
                    down(*expert_before(u, e))
                if e == 0 and not is_late(u):
                    pe.wait_ge(s.in_a, SUBS)
                    pe.wait_ge(s.g_copied, SUBS)
                    router(u.routed)

            def loop(start, end, group):
                peeled(pe, Steps(pe, None), start, end, group)

            spiking_block(sub, loop, experts, lambda u: down(u, E - 1))

        @block.scalar
        def _(act):
            st = Steps(act, s.act_steps)
            activation = nc.scalar.activation

            def silus(u, e):
                for c in range(CHUNKS):
                    act.wait_ge(s.up_ready, u.no * 4 * E + 4 * e + 2 * c + 1)
                    if not (is_first(u.no) and e == 0):
                        act.wait_ge(s.gated, u.no * 2 * E + 2 * e + c - 1)
                    activation(silu[:, c, span(u)], up_banks[c][0][:, span(u)], ACT.Silu).then_inc(s.silu_done, 1)

            def copy_scores(m):
                act.wait_ge(s.router_ps, m + 1)
                if not is_first(m):
                    act.wait_ge(s.comb_done, m)
                activation(scores[:].rearrange("p j e -> p (j e)"), side0[:, SCORES], ACT.Copy)\
                 .then_inc(s.scores_done, 1)

            def start_sum(u, phase1):
                if phase1:
                    act.wait_ge(s.res_done, u.routed + 1)
                else:
                    act.wait_ge(s.x3_done, (u.routed - B + 1) * PER)
                if not is_first(u.no):
                    act.wait_ge(s.added, (u.no - 1) * E + 1)
                activation(first[:, u.place], res[:], ACT.Copy).then_inc(s.sum_started, 1)

            def weigh(u, e):
                act.wait_ge(s.down_ready, u.no * E + e + 1)
                if not (is_first(u.no) and e < 2):
                    act.wait_ge(s.added, u.no * E + e - 1)
                if e == 0:
                    act.wait_ge(s.comb_done, u.routed + 1)
                for j in u.tiles:
                    last = activation(weighted[:, e % 2, j], down_bank[:, j * C:(j + 1) * C], ACT.Copy,
                                      scale=comb[:, u.place, j, e:e + 1])
                last.then_inc(s.y_weighted, 1)

            def router_hi(m, bank):
                act.wait_ge(s.xT_ps, m + 1)
                activation(x_hi[:, place_of(m)], bank[:, 0:N], ACT.Copy).then_inc(s.hi_done, 1)

            def top_weights(m):
                act.wait_ge(s.lead_done, m + 1)
                activation(lead_tanh[:], lead[:], ACT.Tanh, scale=0.5).then_inc(s.tanh_done, 1)
                act.wait_ge(s.tanh_done, m + 1)
                for k in range(TOP):
                    last = activation(top_w[:, k], lead_tanh[:], ACT.Copy, scale=0.5 - k, bias=0.5)
                last.then_inc(s.top_done, 1)

            def copy_xT(b):
                act.wait_ge(s.xnT_ps, b + 1)
                activation(xnT[:], side0[:, 0:N], ACT.Copy).then_inc(s.xnT_done, 1)

            def copy_qkv(b, tiles):
                if not is_first(b):
                    act.wait_ge(s.qT_ps, b)
                for j in tiles:
                    act.wait_ge(s.qkv_ps, b * TILES + j + 1)
                    ps = (side1, side2)[j % 2]
                    activation(qk[:, j].rearrange("p h d -> p (h d)"), ps[:, 0:2 * C], ACT.Relu)
                    activation(v_one[:, j, 0:C], ps[:, 2 * C:3 * C], ACT.Copy).then_inc(s.qkv_out, 1)

            def copy_qT(b):
                act.wait_ge(s.qT_ps, b + 1)
                activation(qT[:], side1[:, 0:N], ACT.Copy).then_inc(s.qT_done, 1)

            def conv_centre(b):
                act.wait_ge(s.att_done, b + 1)
                activation(conv[:], att[:, 1:N + 1], ACT.Identity, scale=centre_w[:, 0:1],
                           bias=cols[:, DWB:DWB + 1]).then_inc(s.conv_mid, 1)

            act.wait_ge(s.load_c, 16 * LOADS_C)
            activation(half_b1[:], cols[:, B1:B1 + FCH], ACT.Copy, scale=HALF)
            activation(half_b2[:], cols[:, B2:B2 + 1], ACT.Copy, scale=HALF)
            st.did(activation(centre_w[:], cols[:, DW + 1:DW + 2], ACT.Copy, bias=1.0))
            st.settle()

            def slot(k, a, c):
                if k == 1 and a is not None:
                    copy_xT(a)
                if k == 2 and a is not None:
                    copy_qkv(a, (0, 1))
                if k == 3 and a is not None:
                    copy_qkv(a, (2, 3))

            def end(a, c, closing):
                if in_lead(a, c) and c is not None:
                    router_hi(c, side2)
                    copy_scores(c)
                    copy_qT(a)
                    return
                if a is not None:
                    copy_qT(a)
                if c is not None:
                    router_hi(c, side2)
                closing()
                if c is not None:
                    copy_scores(c)

            def expert(u, e, beside):
                silus(u, e)
                if e:
                    weigh(u, e - 1)
                else:
                    start_sum(u, True)
                if e == 2 and not (isinstance(u.no, int) and u.no + 1 >= B):
                    conv_centre(u.no + 1)
                if e == 0:
                    top_weights(u.routed)
                beside()

            def lead_in(k):
                if k == 1:
                    conv_centre(0)
                if k == 0:
                    act.wait_ge(s.load_w, 16 * LOADS_W)
                    activation(gate_hi[:], gate_f[:], ACT.Copy)
                    for e in range(E):
                        activation(experts_hi[:, e], experts_f[:, e], ACT.Copy).then_inc(s.hi_split, 1)

            def loop(start, last, batch):
                with act.Fori(start, last) as b:
                    batch(b)

            first_half(lead_in, slot, end, expert, lambda u: weigh(u, E - 1), lambda b, e: None, loop)

            def fill(t, q, first, n, src, **how):
                if not (isinstance(t, int) and t < 1):
                    act.wait_ge(s.lif_steps, t * 2 * STEPS)
                dst = lif_in[:, (q + 1) % 2, first:first + n].rearrange("p a t -> p (a t)")
                return activation(dst, src, ACT.Identity, scale=HALF, **how)

            def sub(t, q, j, on, experts, coming):
                u, e = experts or (None, None)
                r = u.routed if e == 0 and not is_late(u) else None
                if experts:
                    silus(u, e)
                if on.fin:
                    act.wait_ge(s.g_ps, t - LAG_G + 1)
                if on.load:
                    act.wait_ge(s.zT_ps, t + 2)
                    activation(zT[:], side0[:, 0:P], ACT.Copy).then_inc(s.zT_done, 1)
                if on.fin:
                    activation(g_tok[:], side0[:, P:2 * P], ACT.Copy).then_inc(s.g_copied, 1)
                if r is not None:
                    start_sum(u, False)
                if experts and expert_before(u, e):
                    weigh(*expert_before(u, e))
                if r is not None:
                    copy_scores(r)
                if on.load:
                    act.wait_ge(s.rkv_ps, t + 2)
                    fill(t, q, CA, 3 * B, side0[:, 0:3 * P]).then_inc(s.in_a, 1)
                if experts:
                    silus(u, e + 1)
                if on.ffn:
                    act.wait_ge(s.lif2_ps, t - 2)
                    fill(t, q, CC, B, side2[:, 0:P], bias=half_b2[:, 0:1]).then_inc(s.in_c, 1)
                if on.hand:
                    act.wait_ge(s.x1T_ps, t)
                    activation(x1T_ring[:, (q - 1) % PER], side1[:, 0:P], ACT.Identity, scale=cols[:, LN1G:LN1G + 1],
                               bias=cols[:, LN1B:LN1B + 1]).then_inc(s.x1T_done, 1)
                if r is not None:
                    top_weights(r)
                if coming is not None:
                    router_hi(coming, side1)
                if on.hand:
                    act.wait_ge(s.lif1_ps, t)
                    for k in range(FCH):
                        last = fill(t, q, CB + k * B, B, side2[:, k * P:(k + 1) * P], bias=half_b1[:, k:k + 1])
                    last.then_inc(s.in_b, 1)
                if experts:
                    weigh(u, e)

            def experts(u, e):
                silus(u, e)
                if expert_before(u, e):
                    weigh(*expert_before(u, e))
                if e == 0 and not is_late(u):
                    start_sum(u, False)
                    copy_scores(u.routed)
                    top_weights(u.routed)

            def spiking_loop(start, end, group):
                peeled(act, Steps(act, None), start, end, group)

            spiking_block(sub, spiking_loop, experts, lambda u: weigh(u, E - 1))

        @block.gpsimd
        def _(pool):
            st = Steps(pool, s.pool_steps)
            g = nc.gpsimd
            g.memset(minus_half[:], -0.5)
            g.memset(v_one[:, :, C:C + 1], 1.0)
            g.memset(att[:, 0:1], 0.0)
            g.memset(att[:, N + 1:N + 2], 0.0)
            g.memset(lif_in[:], 0.0)
            g.memset(lif_v[:], 0.0)
            g.memset(h_decay[:], DECAY)
            st.did(g.memset(h_out[:], 0.0))
            st.settle()
            g.memset(h_decay[:, :, 0:1], 0.0).then_inc(s.zeros, 1)

            def rstd(ln, k):
                wait_apart(pool, ln.has_var, k + 1)
                st.did(g.tensor_scalar(ln.var[:], ln.mv[:, :, 1], LN_EPS, None, ALU.add))
                st.settle()
                n = ln.var.shape[1]
                g.tensor_tensor(ln.rstd[:], ln.var[:], minus_half[:, 0:n], ALU.pow).then_inc(ln.has_rstd, 1)

            def add(u, e, phase1):
                pool.wait_ge(s.y_weighted, u.no * E + e + 1)
                if e == 0:
                    pool.wait_ge(s.sum_started, u.routed + 1)
                if not (is_first(u.no) and e == 0):
                    pool.wait_ge(s.added, u.no * E + e)
                last = e == E - 1
                if last:
                    if phase1 or is_late(u) or (isinstance(u.no, int) and u.no == UNITS):
                        if not is_first(u.no):
                            pool.wait_ge(s.x2_stored, 16 * u.no)
                            pool.wait_ge(s.z_done, u.no)
                    else:
                        pool.wait_ge(s.out_stored, (u.no - UNITS) * 16 * PER)
                source = acc if e else first[:, u.place]
                g.tensor_tensor(part(moe_out if last else acc, u), part(source, u), part(weighted[:, e % 2], u),
                                ALU.add).then_inc(s.added, 1)

            def add_bias(b):
                pool.wait_ge(s.x_loaded, 16 * (b + 1))
                if not is_first(b):
                    pool.wait_ge(s.res_done, b)
                for j in range(TILES):
                    last = g.tensor_tensor(x_plus_b[:, j], x_tok[:, j], proj_b[:], ALU.add)
                last.then_inc(s.xb_done, 1)

            def cube(b):
                pool.wait_ge(s.qk_first, b + 1)
                st.did(g.tensor_tensor(qk2[:], qk[:], qk[:], ALU.mult))
                st.settle()
                g.tensor_tensor(qk2[:], qk2[:], qk[:], ALU.mult).then_inc(s.cubed, 1)

            def slot(k, a, c):
                if k == 0 and a is not None:
                    if not in_lead(a, c) or c is None:
                        rstd(ln_x, a)
                    if is_first(a):
                        add_bias(a)
                if k == 4 and a is not None:
                    if not in_lead(a, c):
                        cube(a)
                if k == 5 and c is not None:
                    rstd(ln_r, c)
                if k == 7 and is_first(a):
                    rstd(ln_x, 1)
                if k == 6 and a is not None and not is_first(a):
                    add_bias(a)

            def expert(u, e, beside):
                if e:
                    add(u, e - 1, True)
                beside()

            def rest(b, e):
                if e == 2 and not is_first(b):
                    rstd(ln_z, b - 1)

            pool.wait_ge(s.load_c, 16 * LOADS_C)
            def lead_in(k):
                if k != 1:
                    return
                for e in range(E):
                    pool.wait_ge(s.hi_split, e + 1)
                    last = g.tensor_tensor(experts_lo[:, e], experts_f[:, e], experts_hi[:, e].bitcast(fp32),
                                           ALU.subtract)
                last.then_inc(s.lo_split, 1)

            first_half(lead_in, slot, lambda a, c, closing: closing(), expert,
                       lambda u: add(u, E - 1, True), rest,
                       lambda start, last, batch: rounds(pool, st, start, last, batch, 4))
            rstd(ln_z, B - 1)

            def sub(t, q, j, on, experts, coming):
                u, e = experts or (None, None)
                c = t - LAG_G
                if on.fin:
                    place = (q - LAG_G) % PER
                    rstd(ln_g, c)
                if on.hand and coming is None:
                    rstd(ln_a, t - 1)
                if on.fin:
                    pool.wait_ge(s.g_normed, c + 1)
                    st.did(g.tensor_tensor(g_s[:], g_n[:], ln2_g[:], ALU.mult))
                    st.settle()
                    st.did(g.tensor_tensor(g_s[:], g_s[:], ln2_b[:], ALU.add))
                    st.settle()
                    pool.wait_ge(x2_loaded[place], 16 * j)
                    if experts:
                        pool.wait_ge(s.sum_started, u.routed + 1)
                    g.tensor_tensor(res[:, place], g_s[:], x2_ring[:, place], ALU.add).then_inc(s.x3_done, 1)
                if on.hand and coming is not None:
                    rstd(ln_a, t - 1)
                if on.fin:
                    rstd(ln_m, c)
                if isinstance(t, int) and t in LATE_ENDS:
                    rstd(ln_z, B + LATE_ENDS.index(t))
                if experts and expert_before(u, e):
                    add(*expert_before(u, e), False)
                if experts:
                    add(u, e, False)

            def spiking_loop(start, end, group):
                peeled(pool, st, start, end, group)

            def sums(u, e):
                if expert_before(u, e):
                    add(*expert_before(u, e), False)

            spiking_block(sub, spiking_loop, sums,
                          lambda u: add(u, E - 1, False))

        @block.vector
        def _(dve):
            st = Steps(dve, s.dve_steps)
            v = nc.vector

            def gate_product(u, e, c):
                dve.wait_ge(s.silu_done, u.no * 2 * E + 2 * e + c + 1)
                dve.wait_ge(s.up_ready, u.no * 4 * E + 4 * e + 2 * c + 2)
                v.tensor_tensor(hidden[:, e % 2, c, span(u)], silu[:, c, span(u)], up_banks[c][1][:, span(u)], ALU.mult)\
                 .then_inc(s.gated, 1)

            def gate_half(u, e, c, k):
                if k == 0:
                    dve.wait_ge(s.silu_done, u.no * 2 * E + 2 * e + c + 1)
                    dve.wait_ge(s.up_ready, u.no * 4 * E + 4 * e + 2 * c + 2)
                middle = (span(u).start + span(u).stop) // 2
                half = slice(middle, span(u).stop) if k else slice(span(u).start, middle)
                last = v.tensor_tensor(hidden[:, e % 2, c, half], silu[:, c, half], up_banks[c][1][:, half], ALU.mult)
                if k:
                    last.then_inc(s.gated, 1)

            def gate_products(u, e):
                for c in range(CHUNKS):
                    gate_product(u, e, c)

            def stats(ln, src, tiles):
                for j in tiles:
                    ins = v.bn_stats(ln.stats[:, j], src(j))
                st.did(ins)
                st.settle(wait_apart)
                for j in tiles:
                    ins = v.bn_aggr(ln.mv[:, j], ln.stats[:, j])
                ins.then_inc(ln.has_var, 1)

            def normalise(ln, k, dst, src, tiles, done):
                dve.wait_ge(ln.has_rstd, k + 1)
                for j in tiles:
                    ins = v.tensor_scalar(dst(j), src(j), ln.mv[:, j, 0:1], ln.rstd[:, j:j + 1],
                                          ALU.subtract, ALU.mult)
                ins.then_inc(done, 1)

            def router_lo(m, bank):
                dve.wait_ge(s.hi_done, m + 1)
                v.tensor_tensor(x_lo[:, place_of(m)], bank[:, 0:N], x_hi[:, place_of(m)].bitcast(fp32), ALU.subtract).then_inc(s.lo_done, 1)

            def route_steps(m):
                def find():
                    wait_apart(dve, s.scores_done, m + 1)
                    for j in range(TILES):
                        ins = v.max(best[:, j], scores[:, j])
                    st.did(ins)

                def compare():
                    st.settle()
                    v.tensor_tensor(lead[:], best[:, :, 0], best[:, :, 1], ALU.subtract).then_inc(s.lead_done, 1)
                    for j in range(TILES):
                        ins = v.max_index(best_no[:, j], best[:, j], scores[:, j])
                    st.did(ins)

                def number():
                    st.settle()
                    st.did(v.tensor_copy(best_nof[:], best_no[:, :, 0:TOP]))

                def match():
                    st.settle()
                    for k in range(TOP):
                        ins = v.tensor_tensor(pick[:, k], expert_no[:].unsqueeze(1).to_broadcast([P, TILES, E]),
                                              best_nof[:, :, k:k + 1].to_broadcast([P, TILES, E]), ALU.is_equal)
                    st.did(ins)

                def weight():
                    dve.wait_ge(s.top_done, m + 1)
                    st.settle()
                    for k in range(TOP):
                        ins = v.tensor_tensor(pick[:, k], pick[:, k],
                                              top_w[:, k].unsqueeze(2).to_broadcast([P, TILES, E]), ALU.mult)
                    st.did(ins)

                def combine():
                    st.settle()
                    v.tensor_tensor(comb[:, place_of(m)], pick[:, 0], pick[:, 1], ALU.add).then_inc(s.comb_done, 1)

                return [find, compare, number, match, weight, combine]

            def route(m):
                for step in route_steps(m):
                    step()

            def norm_x(b):
                dve.wait_ge(s.x_loaded, 16 * (b + 1))
                stats(ln_x, lambda j: x_tok[:, j], ALL)

            def norm_x2(b):
                if not is_first(b):
                    dve.wait_ge(s.xnT_ps, b)
                normalise(ln_x, b, lambda j: xn[:, j], lambda j: x_tok[:, j], ALL, s.xn_done)

            def merge(t):
                return t[:].rearrange("p j h d -> p (j h) d")

            def inv():
                return qk_inv[:].rearrange("p j h -> p (j h)").unsqueeze(2).to_broadcast([P, TILES * 2 * HEADS, HD])

            def qk_sums(b):
                dve.wait_ge(s.qkv_out, (b + 1) * TILES)
                flat = qk[:].rearrange("p j h d -> p (j h d)")
                st.did(v.tensor_scalar(flat, flat, ATT_EPS, None, ALU.add))
                st.settle()
                st.did(v.tensor_reduce(qk_sum[:], qk[:], axis=AX, op=ALU.add))
                st.settle()
                st.did(v.reciprocal(qk_inv[:], qk_sum[:]))

            def qk_norm(b):
                st.settle()
                v.tensor_tensor(merge(qk), merge(qk), inv(), ALU.mult).then_inc(s.qk_first, 1)

            def cube(b):
                dve.wait_ge(s.qk_first, b + 1)
                st.did(v.tensor_tensor(qk2[:], qk[:], qk[:], ALU.mult))
                st.settle()
                v.tensor_tensor(qk2[:], qk2[:], qk[:], ALU.mult).then_inc(s.cubed, 1)

            def cube_sums(b):
                dve.wait_ge(s.cubed, b + 1)
                st.did(v.tensor_reduce(qk_sum[:], qk2[:], axis=AX, op=ALU.add))
                st.settle()
                v.reciprocal(qk_inv[:], qk_sum[:]).then_inc(s.cubes_inverse, 1)

            def cube_norm(b):
                dve.wait_ge(s.cubes_inverse, b + 1)
                v.tensor_tensor(merge(qk), merge(qk2), inv(), ALU.mult).then_inc(s.qk_done, 1)

            def mask_kv(b):
                dve.wait_ge(s.kv_ps, b + 1)
                if not is_first(b):
                    dve.wait_ge(s.att_ps, b)
                v.tensor_tensor(kv_m[:], side0[:, 0:C], head_mask[:], ALU.mult)
                v.tensor_scalar(ks_m[:], head_mask[:], side0[:, C:C + 1], None, ALU.mult).then_inc(s.kv_masked, 1)

            def add_to_z(b):
                dve.wait_ge(s.att_ps, b + 1)
                v.tensor_scalar(z_inv[:], side0[:, 0:N], ATT_EPS, None, ALU.add).then_inc(s.z_added, 1)

            def invert_z(b):
                dve.wait_ge(s.z_added, b + 1)
                v.reciprocal(z_inv[:], z_inv[:]).then_inc(s.z_inverse, 1)

            def attended(b):
                dve.wait_ge(s.z_inverse, b + 1)
                v.tensor_tensor(att[:, 1:N + 1], side2[:, 0:N], z_inv[:], ALU.mult).then_inc(s.att_done, 1)

            def conv_sides(b):
                dve.wait_ge(s.conv_mid, b + 1)
                st.did(v.scalar_tensor_tensor(conv[:], att[:, 0:N], cols[:, DW:DW + 1], conv[:], ALU.mult, ALU.add))
                st.settle()
                v.scalar_tensor_tensor(conv[:], att[:, 2:N + 2], cols[:, DW + 2:DW + 3], conv[:], ALU.mult, ALU.add)\
                 .then_inc(s.conv_done, 1)

            def residual(b):
                dve.wait_ge(s.proj_ps, b + 1)
                dve.wait_ge(s.xb_done, b + 1)
                if not is_first(b):
                    dve.wait_ge(s.sum_started, b)
                v.tensor_tensor(res[:].rearrange("p j c -> p (j c)"), side1[:, 0:N],
                                x_plus_b[:].rearrange("p j c -> p (j c)"), ALU.add).then_inc(s.res_done, 1)
                dve.wait_ge(s.res_done, b + 1)
                stats(ln_r, lambda j: res[:, j], ALL)

            def norm_res(b):
                if not is_first(b):
                    dve.wait_ge(s.xT_ps, b)
                normalise(ln_r, b, lambda j: resn[:, j], lambda j: res[:, j], ALL, s.resn_done)

            def norm_out_stats(u):
                dve.wait_ge(s.added, (u.no + 1) * E)
                stats(ln_z, lambda j: moe_out[:, j], u.tiles)

            def norm_out(u):
                if not is_first(u.no):
                    dve.wait_ge(s.z_stored, 16 * u.no)
                normalise(ln_z, u.no, lambda j: z_tok[:, j], lambda j: moe_out[:, j], u.tiles, s.z_done)

            def slot(k, a, c):
                lead = in_lead(a, c)
                if k == 0:
                    if lead and c is not None:
                        norm_x2(a)
                    if c is not None:
                        add_to_z(c)
                    if is_first(a):
                        norm_x(a)
                if k == 1:
                    if is_first(a):
                        norm_x2(a)
                    if c is not None:
                        invert_z(c)
                        attended(c)
                if k == 3:
                    if c is not None:
                        conv_sides(c)
                    if a is not None:
                        qk_sums(a)
                if lead:
                    lead_slot(k, a, c)
                    return
                if k == 4 and a is not None:
                    qk_norm(a)
                if k == 5 and c is not None:
                    residual(c)
                if k == 6:
                    if a is not None:
                        cube_sums(a)
                    if c is not None:
                        norm_res(c)

            def lead_slot(k, a, c):
                if k == 4:
                    if c is not None:
                        residual(c)
                    qk_norm(a)
                    if c is not None:
                        norm_res(c)
                    cube(a)
                    if c is not None:
                        router_lo(c, side2)
                if k == 6:
                    cube_sums(a)
                if k == 7:
                    cube_norm(a)
                    if is_first(a):
                        norm_x(1)

            def end(a, c, closing):
                if a is not None:
                    mask_kv(a)
                if c is not None and not in_lead(a, c):
                    router_lo(c, side2)
                closing()

            def expert(u, e, beside):
                if not (isinstance(u.no, int) and u.no + 2 >= B):
                    if e == 1:
                        norm_x2(u.no + 2)
                    if e == E - 1:
                        cube_norm(u.no + 2)
                gate_products(u, e)
                if e == 0:
                    if not (isinstance(u.no, int) and u.no + 2 >= B):
                        norm_x(u.no + 2)
                    route(u.routed)
                beside()

            def split_lif2():
                st.did(v.tensor_copy(lif2_part[:, 0], lif2_f[:]))
                st.settle()
                st.did(v.tensor_tensor(lif2_rest[:], lif2_f[:], lif2_part[:, 0], ALU.subtract))
                st.settle()
                st.did(v.tensor_copy(lif2_part[:, 1], lif2_rest[:]))
                st.settle()
                st.did(v.tensor_tensor(lif2_rest[:], lif2_rest[:], lif2_part[:, 1], ALU.subtract))
                st.settle()
                v.tensor_copy(lif2_part[:, 2], lif2_rest[:]).then_inc(s.lo_split, 1)

            def rest(b, e):
                if not is_first(b):
                    if e == 2:
                        norm_out_stats(unit_of_batch(b - 1))
                    if e == 4:
                        norm_out(unit_of_batch(b - 1))
                    if e == 5 and isinstance(b, int) and b == B - 1:
                        split_lif2()

            def lead_in(k):
                if k != 3:
                    return
                dve.wait_ge(s.hi_split, E)
                v.tensor_tensor(gate_lo[:], gate_f[:], gate_hi[:].bitcast(fp32), ALU.subtract)\
                 .then_inc(s.lo_split, 1)

            dve.wait_ge(s.zeros, 1)
            dve.wait_ge(s.load_c, 16 * LOADS_C)
            first_half(lead_in, slot, end, expert, lambda b: None, rest,
                       lambda start, last, batch: rounds(dve, st, start, last, batch, 13))
            norm_out_stats(EARLY[-1])

            def sub(t, q, j, on, experts, coming):
                if not on.scan and not on.fin:
                    return
                now, old = lif_u[:, q % 2], lif_u[:, (q + 1) % 2]
                source = lif_in[:, q % 2]
                u, e = experts or (None, None)

                def carry_in():
                    v.tensor_copy(kv_in[:, :, 0:1], h_out[:, :, STEPS:STEPS + 1])
                    st.did(v.tensor_scalar(v_spike[:], old[:, 2 * B:3 * B], V_TH, None, ALU.is_ge))

                def spikes_kv():
                    st.settle()
                    st.did(v.scalar_tensor_tensor(kv_in[:, :, 1:], old[:, B:2 * B], V_TH, v_spike[:],
                                                  ALU.is_ge, ALU.mult))

                def scan_h():
                    st.settle()
                    st.did(v.tensor_tensor_scan(h_out[:].rearrange("p b t -> p (b t)"),
                                                h_decay[:].rearrange("p b t -> p (b t)"),
                                                kv_in[:].rearrange("p b t -> p (b t)"), 0.0, ALU.mult, ALU.add))

                def gate_h():
                    st.settle()
                    if not (isinstance(t, int) and t < 2):
                        dve.wait_ge(s.wo_ps, t - 1)
                    v.scalar_tensor_tensor(y_fm[:].rearrange("p (b t) -> p b t", b=B), old[:, 0:B], V_TH,
                                           h_out[:, :, 1:], ALU.is_ge, ALU.mult).then_inc(s.y_done, 1)

                def ffn_spikes():
                    if not (isinstance(t, int) and t < 4):
                        dve.wait_ge(s.lif2_ps, t - 3)
                    v.tensor_scalar(s1[:].rearrange("p k t -> p (k t)"),
                                    old[:, CB:CB + FCH * B].rearrange("p a t -> p (a t)"), V_TH, None, ALU.is_ge)\
                     .then_inc(s.s1_done, 1)

                def final_sum():
                    if not (isinstance(t, int) and t < LAG_G + 1):
                        dve.wait_ge(s.g_ps, t - LAG_G)
                    v.scalar_tensor_tensor(gT[:], old[:, CC:CC + B].rearrange("p a t -> p (a t)"), V_TH,
                                           x1T_ring[:, (q - LAG_G) % PER], ALU.is_ge, ALU.add).then_inc(s.g_done, 1)

                def x1_sum():
                    dve.wait_ge(s.wo_ps, t)
                    v.tensor_tensor(x1p[:], side1[:, 0:C], z_ring[:, (q - 1) % PER], ALU.add).then_inc(s.x1p_done, 1)

                def x1_stats():
                    dve.wait_ge(s.x1p_done, t)
                    st.did(v.bn_stats(ln_a.stats[:, 0], x1p[:]))

                def x1_aggr():
                    st.settle(wait_apart)
                    v.bn_aggr(ln_a.mv[:, 0], ln_a.stats[:, 0]).then_inc(ln_a.has_var, 1)

                def x1_norm():
                    normalise(ln_a, t - 1, lambda j: x1n[:], lambda j: x1p[:], (0,), s.x1n_done)

                def g_stats():
                    dve.wait_ge(s.g_copied, t - LAG_G + 1)
                    st.did(v.bn_stats(ln_g.stats[:, 0], g_tok[:]))

                def g_aggr():
                    st.settle(wait_apart)
                    v.bn_aggr(ln_g.mv[:, 0], ln_g.stats[:, 0]).then_inc(ln_g.has_var, 1)

                def g_norm():
                    normalise(ln_g, t - LAG_G, lambda j: g_n[:], lambda j: g_tok[:], (0,), s.g_normed)

                def m_stats():
                    dve.wait_ge(s.x3_done, t - LAG_G + 1)
                    st.did(v.bn_stats(ln_m.stats[:, 0], res[:, (q - LAG_G) % PER]))

                def m_aggr():
                    st.settle(wait_apart)
                    v.bn_aggr(ln_m.mv[:, 0], ln_m.stats[:, 0]).then_inc(ln_m.has_var, 1)

                def m_norm():
                    place = (q - LAG_G) % PER
                    normalise(ln_m, t - LAG_G, lambda j: resn[:, place], lambda j: res[:, place], (0,), s.x3n_done)

                fill = []

                def at(slot, *ops):
                    fill.append((slot, ops))

                def at_gate(first_slot, second_slot, u, e, c):
                    at(first_slot, lambda: gate_half(u, e, c, 0))
                    at(second_slot, lambda: gate_half(u, e, c, 1))

                if on.fin:
                    at(0, final_sum)
                if on.hand:
                    at(1, carry_in)
                    at(2, spikes_kv)
                    at(3, scan_h)
                    at(4, gate_h)
                if experts:
                    at_gate(5, 6, u, e, 0)
                    at_gate(9, 11, u, e, 1)
                if on.fin:
                    at(7, g_stats)
                    at(8, g_aggr)
                    at(14 if coming is None else 12, g_norm)
                    at(19 if coming is None else 17, m_stats)
                    at(20 if coming is None else 19, m_aggr)
                    at(24 if coming is None else 23, m_norm)
                if on.hand:
                    at(10, x1_sum)
                    at(12 if coming is None else 13, x1_stats)
                    at(13 if coming is None else 14, x1_aggr)
                    at(17 if coming is None else 20, x1_norm)
                if on.ffn:
                    at(15, ffn_spikes)
                if experts and (e or is_late(u)):
                    at_gate(16, 18, u, e + 1, 0)
                    at_gate(21, 22, u, e + 1, 1)
                elif experts:
                    for slot, step in zip((19, 21, 22, 26, 28, 31), route_steps(u.routed)):
                        at(slot, step)
                    at_gate(23, 25, u, e + 1, 0)
                    at_gate(29, 30, u, e + 1, 1)
                if isinstance(t, int) and t in LATE_ENDS:
                    late = LATE[LATE_ENDS.index(t)]
                    at(20, lambda: norm_out_stats(late))
                    at(31, lambda: norm_out(late))
                if coming is not None:
                    at(29, lambda: router_lo(coming, side1))

                def side(slot):
                    for when, ops in fill:
                        if when == slot:
                            for op in ops:
                                op()

                begun = CA + 3 * B if isinstance(t, int) and t < 2 else CC if isinstance(t, int) and t < 4 else COLS
                if on.load or on.hand:
                    dve.wait_ge(s.in_a, upto(t + 1))
                if not (isinstance(t, int) and t < 2):
                    dve.wait_ge(s.in_b, upto(t - 1))
                if not (isinstance(t, int) and t < 4):
                    dve.wait_ge(s.in_c, upto(t - 3))
                for i in range(STEPS):
                    if on.scan:
                        if not (i == 0 and is_first(t)):
                            dve.wait_ge(s.lif_steps, t * 2 * STEPS + 2 * i)
                        v.scalar_tensor_tensor(now[:, :begun, i], lif_v[:, :begun], HALF, source[:, :begun, i],
                                               ALU.mult, ALU.add)\
                         .then_inc(s.lif_steps, 1)
                    side(2 * i)
                    if on.scan:
                        dve.wait_ge(s.lif_steps, t * 2 * STEPS + 2 * i + 1)
                        v.scalar_tensor_tensor(lif_v[:, :begun], now[:, :begun, i], V_TH, now[:, :begun, i],
                                               ALU.is_lt, ALU.mult)\
                         .then_inc(s.lif_steps, 1)
                    side(2 * i + 1)

            def experts_alone(u, e):
                gate_products(u, e)
                if e == 0:
                    if is_late(u):
                        norm_out(EARLY[-1])
                    else:
                        route(u.routed)

            def spiking_loop(start, end, group):
                peeled(dve, st, start, end, group)

            spiking_block(sub, spiking_loop, experts_alone, lambda u: None)

    return nc


def kernel(**inputs):
    import numpy as np
    import concourse.bacc as bacc
    from concourse.bass_utils import run_bass_kernel_spmd

    a, b, f = "L0_attn_a_", "L0_attn_b_", "L0_ffn_"
    given = {k: np.asarray(v) for k, v in inputs.items()}
    p = np.arange(128)

    def columns(v):
        return v.reshape(-1, 128).T

    arrays = {
        "x": given[a + "x"],
        "qkv_w": given[a + "w_qkv"].T,
        "proj_w": given[a + "w_proj"].T,
        "b_proj": given[a + "b_proj"],
        "wr": given[b + "Wr"].T,
        "wk": given[b + "Wk"].T,
        "wv": given[b + "Wv"].T,
        "wo": given[b + "Wo"].T,
        "lif_w1": given[b + "W1"].T,
        "lif_w2": given[b + "W2"].T,
        "ln2_g": given[b + "ln2_g"],
        "ln2_b": given[b + "ln2_b"],
        "Wg": given[f + "Wg"],
        "W1": given[f + "W1"],
        "W3": given[f + "W3"],
        "W2": given[f + "W2"],
        "cols": np.concatenate([columns(given[b + "b1"]), columns(given[b + "b2"]), columns(given[b + "ln1_g"]),
                                columns(given[b + "ln1_b"]), given[a + "w_dwc"], columns(given[a + "b_dwc"])],
                               axis=1),
        "ident": np.eye(128, dtype=np.float32),
        "head_mask": (p[:, None] // 8 == p[None, :] // 8).astype(np.float32),
        "expert_no": np.tile(np.arange(8, dtype=np.float32), (128, 1)),
    }
    arrays = {k: np.ascontiguousarray(v) for k, v in arrays.items()}
    nc = bacc.Bacc("TRN2", target_bir_lowering=False, num_devices=1)
    dram, feeds = {}, {}
    for name, value in arrays.items():
        dram[name] = nc.dram_tensor(f"in_{name}", value.shape, mybir.dt.from_np(value.dtype),
                                    kind="ExternalInput").ap()
        feeds[f"in_{name}"] = value
    dram["out"] = nc.dram_tensor("out_x", arrays["x"].shape, mybir.dt.float32, kind="ExternalOutput").ap()
    build_program(nc, dram)
    done = run_bass_kernel_spmd(nc, [feeds], core_ids=[0])
    return done.results[0]["out_x"]
```
